# Optimizing a Trainium2 kernel written in Bass

```python
import numpy as np
import jax
import jax.numpy as jnp

def _softmax(x, axis=-1):
    return jax.nn.softmax(x, axis=axis)

def _gelu(x):
    return jax.nn.gelu(x, approximate=True)

def _silu(x):
    return jax.nn.silu(x)

def _sigmoid(x):
    return jax.nn.sigmoid(x)

def _layernorm(x, axis=-1, eps=1e-05):
    m = jnp.mean(x, axis=axis, keepdims=True)
    v = jnp.var(x, axis=axis, keepdims=True)
    return (x - m) / jnp.sqrt(v + eps)

def _scatter_add(tgt, idx, src, axis=0):
    return tgt.at[idx].add(src)

def _segment_sum(src, seg, n):
    return jax.ops.segment_sum(src, seg, n)
kernel_name = 'mk_gnn_preln_d2_gnn_r32_54ad1f'

def setup_inputs(seed: int=0):
    np.random.seed(seed)
    _w = jnp.asarray

    def _rec_inputs():
        import jax
        import jax.numpy as jnp
        _gk = jax.random.key(seed)
        x = -0.0003713 + 1 * jax.random.normal(jax.random.fold_in(_gk, 1), (3125, 128), jnp.float32)
        src = jax.random.randint(jax.random.fold_in(_gk, 2), (100000,), 0, 3125, jnp.int32)
        dst = jax.random.randint(jax.random.fold_in(_gk, 3), (100000,), 0, 3125, jnp.int32)
        _o = jnp.argsort(dst, stable=True)
        src = src[_o]
        dst = dst[_o]
        edge_attr_64 = -5.3897e-05 + 0.999841 * jax.random.normal(jax.random.fold_in(_gk, 12), (100000, 64), jnp.float32)
        edge_weight = jax.random.uniform(jax.random.fold_in(_gk, 13), (100000,), jnp.float32, 0.0, 0.999998)
        edge_weight_n2 = jax.random.uniform(jax.random.fold_in(_gk, 14), (100000,), jnp.float32, 0.0, 0.999998)
        return (x, src, dst, edge_attr_64, edge_weight, edge_weight_n2)
    x, src, dst, edge_attr_64, edge_weight, edge_weight_n2 = _rec_inputs()

    def _L0_gnn_setup():
        import jax, jax.numpy as jnp
        import numpy as np
        N_NODES, N_EDGES = (3125, 12500)
        D_NODE, D_EDGE, N_COND, N_ROUNDS = (128, 64, 2, 3)

        def gru_cell(x, h, Wih, Whh, bih, bhh):
            gi = x @ Wih.T + bih
            gh = h @ Whh.T + bhh
            ir, iz, inn = jnp.split(gi, 3, axis=-1)
            hr, hz, hn = jnp.split(gh, 3, axis=-1)
            r = jax.nn.sigmoid(ir + hr)
            z = jax.nn.sigmoid(iz + hz)
            n = jnp.tanh(inn + r * hn)
            return (1.0 - z) * n + z * h
        key = jax.random.key(seed)
        ks = jax.random.split(key, 10)
        scale = jnp.float32(0.05)
        d_in = 2 * D_NODE + D_EDGE + N_COND
        h = jax.random.normal(ks[0], (N_NODES, D_NODE), jnp.float32)
        e = jax.random.normal(ks[1], (N_EDGES, D_EDGE), jnp.float32)
        src = jax.random.randint(ks[2], (N_EDGES,), 0, N_NODES)
        dst = jax.random.randint(ks[3], (N_EDGES,), 0, N_NODES)
        cond = jax.random.normal(ks[4], (N_COND,), jnp.float32)
        U_W = jax.random.normal(ks[5], (N_ROUNDS, D_NODE, d_in), jnp.float32) * scale
        U_b = jnp.zeros((N_ROUNDS, D_NODE), jnp.float32)
        Wih = jax.random.normal(ks[6], (N_ROUNDS, 3 * D_NODE, D_NODE), jnp.float32) * scale
        Whh = jax.random.normal(ks[7], (N_ROUNDS, 3 * D_NODE, D_NODE), jnp.float32) * scale
        bih = jnp.zeros((N_ROUNDS, 3 * D_NODE), jnp.float32)
        bhh = jnp.zeros((N_ROUNDS, 3 * D_NODE), jnp.float32)
        return dict(h=h, e=e, src=src, dst=dst, cond=cond, U_W=U_W, U_b=U_b, Wih=Wih, Whh=Whh, bih=bih, bhh=bhh)
    _L0_gnn_all = _L0_gnn_setup()
    _L0_gnn_in = {k: v for k, v in _L0_gnn_all.items() if k in ('cond', 'U_W', 'U_b', 'Wih', 'Whh', 'bih', 'bhh')}
    del _L0_gnn_all

    def _L1_gnn_setup():
        import jax, jax.numpy as jnp
        import numpy as np
        N_NODES = 50000
        N_EDGES = 18750
        D_FEAT = 128
        key = jax.random.key(seed)
        k_h, k_src, k_dst, k_dt, k_norm = jax.random.split(key, 5)
        h = jax.random.normal(k_h, (N_NODES, D_FEAT), dtype=jnp.float32)
        src = jax.random.randint(k_src, (N_EDGES,), 0, N_NODES, dtype=jnp.int32)
        dst = jax.random.randint(k_dst, (N_EDGES,), 0, N_NODES, dtype=jnp.int32)
        dt = jax.random.uniform(k_dt, (N_EDGES,), dtype=jnp.float32) * 10.0
        norm = jax.random.uniform(k_norm, (N_EDGES,), dtype=jnp.float32)
        decay_lam = jnp.full((1,), 0.1, dtype=jnp.float32)
        return {'h': h, 'src': src, 'dst': dst, 'dt': dt, 'norm': norm, 'decay_lam': decay_lam}
    _L1_gnn_all = _L1_gnn_setup()
    _L1_gnn_in = {k: v for k, v in _L1_gnn_all.items() if k in ('decay_lam',)}
    del _L1_gnn_all
    return {'x': x, 'src': src, 'dst': dst, 'edge_attr_64': edge_attr_64, 'edge_weight': edge_weight, 'edge_weight_n2': edge_weight_n2, 'L0_gnn_cond': _L0_gnn_in['cond'], 'L0_gnn_U_W': _L0_gnn_in['U_W'], 'L0_gnn_U_b': _L0_gnn_in['U_b'], 'L0_gnn_Wih': _L0_gnn_in['Wih'], 'L0_gnn_Whh': _L0_gnn_in['Whh'], 'L0_gnn_bih': _L0_gnn_in['bih'], 'L0_gnn_bhh': _L0_gnn_in['bhh'], 'L1_gnn_decay_lam': _L1_gnn_in['decay_lam']}

def reference(x, src, dst, edge_attr_64, edge_weight, edge_weight_n2, L0_gnn_cond, L0_gnn_U_W, L0_gnn_U_b, L0_gnn_Wih, L0_gnn_Whh, L0_gnn_bih, L0_gnn_bhh, L1_gnn_decay_lam):
    import jax
    import jax.numpy as jnp

    def _L0_gnn_ref(h, e, src, dst, cond, U_W, U_b, Wih, Whh, bih, bhh):
        import jax, jax.numpy as jnp
        import numpy as np
        N_NODES, N_EDGES = (3125, 12500)
        D_NODE, D_EDGE, N_COND, N_ROUNDS = (128, 64, 2, 3)

        def gru_cell(x, h, Wih, Whh, bih, bhh):
            gi = x @ Wih.T + bih
            gh = h @ Whh.T + bhh
            ir, iz, inn = jnp.split(gi, 3, axis=-1)
            hr, hz, hn = jnp.split(gh, 3, axis=-1)
            r = jax.nn.sigmoid(ir + hr)
            z = jax.nn.sigmoid(iz + hz)
            n = jnp.tanh(inn + r * hn)
            return (1.0 - z) * n + z * h
        n_nodes = h.shape[0]
        n_edges = e.shape[0]
        cond_e = jnp.broadcast_to(cond, (n_edges, cond.shape[0]))
        for k in range(U_W.shape[0]):
            x = jnp.concatenate([h[dst], h[src], e, cond_e], axis=-1)
            msg = x @ U_W[k].T + U_b[k]
            agg = jax.ops.segment_sum(msg, dst, num_segments=n_nodes)
            h = gru_cell(agg, h, Wih[k], Whh[k], bih[k], bhh[k])
        return h

    def _L1_gnn_ref(h, src, dst, dt, norm, decay_lam):
        import jax, jax.numpy as jnp
        import numpy as np
        N_NODES = 50000
        N_EDGES = 18750
        D_FEAT = 128
        lam = jax.nn.relu(decay_lam[0]) + 0.0001
        w = norm * jnp.exp(-lam * dt)
        m = h[src] * w[:, None]
        h_new = jax.ops.segment_sum(m, dst, num_segments=h.shape[0])
        return h_new
    h = jnp.maximum(_layernorm(x, axis=-1), 0.0)
    x = x + _L0_gnn_ref(h, edge_attr_64, src, dst, L0_gnn_cond, L0_gnn_U_W, L0_gnn_U_b, L0_gnn_Wih, L0_gnn_Whh, L0_gnn_bih, L0_gnn_bhh)
    h = jnp.maximum(_layernorm(x, axis=-1), 0.0)
    x = x + _L1_gnn_ref(h, src, dst, edge_weight, edge_weight_n2, L1_gnn_decay_lam)
    return x

_drawn_inputs = setup_inputs


def setup_inputs(seed=0):
    import zlib

    import numpy as np

    out = dict(_drawn_inputs(seed))
    spreads = {'L0_gnn_U_b': (0.0, 0.1), 'L0_gnn_bih': (0.0, 0.302), 'L0_gnn_bhh': (0.0, 0.394)}
    factors = {'edge_weight': 6.286}
    for name, (base, spread) in spreads.items():
        noise = np.random.default_rng([zlib.crc32(name.encode()), seed]).standard_normal(out[name].shape)
        drawn = base * np.exp(spread * noise) if base else spread * noise
        out[name] = jnp.asarray(drawn.astype(out[name].dtype))
    for name, factor in factors.items():
        out[name] = (out[name] * factor).astype(out[name].dtype)
    return out
```

```python
import concourse.bass as bass
from concourse import mybir
from contextlib import ExitStack

N, E, F, FE = 3125, 100000, 128, 64
ROUNDS = 3
P = 128
HI = -(-N // P)
NP = HI * P
WD = 8
KEYS = WD * HI
NWIN = NP // WD
BD = 64
WPB = BD // WD
NBLK = NP // BD
BCOLS = HI * BD
NCH = -(-E // P)
CT = -(-NCH // P)
NCP = CT * P
FULLCH = E // P
STEP = 3
WT = 4
WPT = NWIN // WT
GE = 512
GJ = GE // P
NG = 200
GT = 2
GPT = NG // GT
FULLG = E // GE
GTAIL = E - FULLG * GE
SW = 32
EA = FE + 1
ERING = 8
NODST = 4095
BIG = 1024.0
HALF = 320
HB = HALF // BD
NHALF = NP // HALF
NSUP = NHALF // 2
EPS = 1e-5


def build(nc, x, src, dst, edge_attr, dt_in, norm_in, cond, U_W, U_b, Wih, Whh, bih, bhh, lam, out):
    f32, bf16, i32 = mybir.dt.float32, mybir.dt.bfloat16, mybir.dt.int32
    f16 = mybir.dt.float16
    ALU, ACT, AX = mybir.AluOpType, mybir.ActivationFunctionType, mybir.AxisListType

    ctx = ExitStack()
    with ctx:
        def sb(name, shape, dt=f32):
            return ctx.enter_context(nc.sbuf_tensor(name, shape, dt))

        def pb(name, shape):
            return ctx.enter_context(nc.psum_tensor(name, shape, f32))

        def sem(name):
            return ctx.enter_context(nc.semaphore(name))

        count_dram = nc.dram_tensor("count_dram", [NBLK, P, BCOLS], f32, kind="Internal").ap()
        wsum_dram = nc.dram_tensor("wsum_dram", [NBLK, P, BCOLS], f32, kind="Internal").ap()

        ident = sb("ident", [P, P])
        ones = sb("ones", [P, P])
        x_nat = sb("x_nat", [P, HI, F])
        h_nat = sb("h_nat", [P, HI, F])
        hT = sb("hT", [P, NP])
        degB = sb("degB", [P, NP])
        sumE = sb("sumE", [EA, NP + SW])
        stats = sb("stats", [P, HI, 6])
        mv = sb("mv", [P, HI, 2])
        rstd = sb("rstd", [P, HI])

        loT = sb("loT", [P, NCP])
        keyT = sb("keyT", [P, NCP])
        wT = [sb(f"w{q}T", [P, NCP]) for q in range(3)]
        winTab = sb("winTab", [1, 3, NWIN], i32)
        grpTab = sb("grpTab", [1, 3, NG], i32)
        iotaLo = sb("iotaLo", [P, P], f16)
        iotaKey = sb("iotaKey", [P, WPB * KEYS], f16)
        blkBase = sb("blkBase", [P, NBLK])
        iotaS = sb("iotaS", [P, SW])
        further = sb("further", [P, N // SW + 1])
        dstG = sb("dstG", [P, NG, GJ])

        AREA = 16700
        area = sb("area", [P, AREA])

        def carve(at, cols, dt=f32):
            v = area[:, at:at + cols]
            return v if dt == f32 else v.bitcast(dt)

        ROW = CT * P
        rowDst = carve(0, ROW, i32).rearrange("p (t e) -> p t e", t=CT)
        rowSrc = carve(ROW, ROW, i32).rearrange("p (t e) -> p t e", t=CT)
        rowDt = carve(2 * ROW, ROW).rearrange("p (t e) -> p t e", t=CT)
        rowNorm = carve(3 * ROW, ROW).rearrange("p (t e) -> p t e", t=CT)
        rowHi = carve(4 * ROW, ROW, i32).rearrange("p (t e) -> p t e", t=CT)
        rowLoI = carve(5 * ROW, ROW, i32).rearrange("p (t e) -> p t e", t=CT)
        rowLo = carve(6 * ROW, ROW).rearrange("p (t e) -> p t e", t=CT)
        rowKey = carve(7 * ROW, ROW).rearrange("p (t e) -> p t e", t=CT)
        rowW = carve(8 * ROW, ROW).rearrange("p (t e) -> p t e", t=CT)
        rowG = carve(9 * ROW, GT * GE, i32).rearrange("p (t e) -> p t e", t=GT)
        rowGf = carve(9 * ROW + GT * GE, GT * GE).rearrange("p (t e) -> p t e", t=GT)
        a0 = 9 * ROW + 2 * GT * GE
        diag = carve(a0, 2 * P).rearrange("p (k c) -> p k c", k=2)
        chMinB = carve(0, NCP)
        chMaxB = carve(NCP, NCP)
        m0 = carve(2 * NCP, NCP)
        m1 = carve(3 * NCP, NCP)
        cLess = carve(4 * NCP, NCP)
        cPlus = carve(5 * NCP, NCP)
        wres = carve(a0 + 256, NCP)
        wbf = carve(a0 + 256 + NCP, NCP // 2, bf16)
        assert a0 + 256 + NCP + NCP // 2 <= AREA
        chMM = sb("chMM", [P, 2, CT], i32)
        chMMf = sb("chMMf", [P, 2, CT])
        gMM = sb("gMM", [P, 2, GT], i32)
        gMMf = sb("gMMf", [P, 2, GT])
        gMMi = sb("gMMi", [P, 2, GT], i32)
        winId = sb("winId", [P, WT])
        loHi = sb("loHi", [P, 2, WT])
        rowTab = sb("rowTab", [1, 4, NWIN])
        zrow = sb("zrow", [1, NWIN])
        lamB = sb("lamB", [P, 1])
        lamN = sb("lamN", [P, 1])
        condB = sb("condB", [P, 2])

        at = 0

        def take(cols, dt=f32):
            nonlocal at
            v = carve(at, cols, dt)
            at += cols
            return v
        hot = [[take(STEP * P // 2, bf16).rearrange("p (j c) -> p j c", j=STEP) for _ in range(4)] for _ in range(2)]
        key = [take(STEP * KEYS // 2, bf16).rearrange("p (j c) -> p j c", j=STEP) for _ in range(2)]
        xhot = [take(P // 2, bf16) for _ in range(4)]
        xkey = take(KEYS // 2, bf16)
        stageC = [take(BCOLS).rearrange("p (s d) -> p s d", s=HI) for _ in range(2)]
        stageW = [take(BCOLS).rearrange("p (s d) -> p s d", s=HI) for _ in range(2)]
        ehot = [take(GJ * SW).rearrange("p (j c) -> p j c", j=GJ) for _ in range(2)]
        exhot = take(GJ * SW).rearrange("p (j c) -> p j c", j=GJ)
        exrel = take(GJ)
        assert at <= AREA
        ebuf = sb("ebuf", [P, ERING, GJ, EA])

        at = 0
        strm = [take(HB * BCOLS).rearrange("p (b s d) -> p b s d", b=HB, s=HI) for _ in range(2)]
        assert at <= AREA
        agg0 = [sb(f"agg0{c}", [P, HALF]) for c in range(2)]
        hdeg = [sb(f"hdeg{c}", [P, HALF]) for c in range(2)]
        agg = [sb(f"agg{c}", [P, HALF]) for c in range(2)]
        gate = sb("gate", [P, 4, HALF])
        wnat = ebuf[:, :, :, :].rearrange("p a b c -> p (a b c)")
        unat = wnat[:, 0:2 * F + FE + 2]
        ihnat = wnat[:, 512:512 + 3 * F].rearrange("p (g c) -> p g c", g=3)
        hhnat = wnat[:, 1024:1024 + 3 * F].rearrange("p (g c) -> p g c", g=3)
        cbv = sb("cbv", [P, 4])
        bnat = sb("bnat", [P, 7])
        brz = sb("brz", [P, 2])
        eaw = sb("eaw", [P, F])
        wts = sb("wts", [P, 9, F])

        bank = [pb(f"bank{i}", [P, 512]) for i in range(8)]
        psC, psW, psE, psX = bank[0:2], bank[2:4], bank[4:6], bank[6]
        psP, psM, psR, psZ, psI, psH, psT = bank[0:2], bank[2], bank[3], bank[4], bank[5], bank[6], bank[7]

        const_ready = sem("const_ready")
        pad_ready = sem("pad_ready")
        rows_in = sem("rows_in")
        small_in = sem("small_in")
        xpad_ready = sem("xpad_ready")
        x_in = sem("x_in")
        lam_ready = sem("lam_ready")
        decay_ready = sem("decay_ready")
        rows_ready = sem("rows_ready")
        step_done = sem("step_done")
        tab_turned = sem("tab_turned")
        tab_out = sem("tab_out")
        diag_ready = sem("diag_ready")
        diag_spread = sem("diag_spread")
        spread_out = sem("spread_out")
        lohi_ready = sem("lohi_ready")
        grp_turned = sem("grp_turned")
        lohi_turned = sem("lohi_turned")
        tables_ready = sem("tables_ready")
        var_ready = sem("var_ready")
        std_ready = sem("std_ready")
        norm_ready = sem("norm_ready")
        e_in = [sem(f"e_in{r}") for r in range(ERING)]
        ehot_ready = sem("ehot_ready")
        e_used = sem("e_used")
        e_added = sem("e_added")
        exrel_ready = sem("exrel_ready")
        exhot_ready = sem("exhot_ready")
        ex_done = sem("ex_done")
        ex_added = sem("ex_added")
        hot01_ready = sem("hot01_ready")
        hot2_ready = sem("hot2_ready")
        hot3_ready = sem("hot3_ready")
        win_done = sem("win_done")
        xhot_ready = sem("xhot_ready")
        xhot_used = sem("xhot_used")
        count_out = sem("count_out")
        wsum_out = sem("wsum_out")
        count_stored = [sem(f"count_stored{c}") for c in range(2)]
        wsum_stored = [sem(f"wsum_stored{c}") for c in range(2)]
        count_stages = sem("count_stages")
        wsum_stages = sem("wsum_stages")
        deg_spread = sem("deg_spread")
        deg_out = sem("deg_out")
        strm_in = [sem(f"strm_in{c}") for c in range(2)]
        prod_done = sem("prod_done")
        prod_out = sem("prod_out")
        hdeg_ready = sem("hdeg_ready")
        msg_done = sem("msg_done")
        agg_ready = sem("agg_ready")
        gates_done = sem("gates_done")
        rz_ready = sem("rz_ready")
        cand_in = sem("cand_in")
        cand_ready = sem("cand_ready")
        gru_step = sem("gru_step")
        h_ready = sem("h_ready")
        w_in = sem("w_in")
        w_prep = sem("w_prep")
        w_turned = sem("w_turned")
        w_ready = sem("w_ready")
        t_done = sem("t_done")
        t_out = sem("t_out")
        res_ready = sem("res_ready")
        out_stored = sem("out_stored")

        AHEAD = 2
        NTB = -(-HI // 4)
        NBODY = NBLK // 2
        WPG = 2 * WPB // ERING

        def batch(b):
            return 4 * b, min(4, HI - 4 * b)

        def wait(eng, s, v):
            if not (isinstance(v, int) and v <= 0):
                eng.wait_ge(s, v)

        block = ctx.enter_context(nc.Block())

        @block.sync
        def _(sp):
            sp.wait_ge(pad_ready, 2)
            whole = (CT - 1) * P * P
            k = FULLCH - (CT - 1) * P
            for rows, dram in ((rowDst, dst), (rowSrc, src), (rowDt, dt_in), (rowNorm, norm_in)):
                sp.dma_start(rows[:, 0:CT - 1, :],
                             dram[0:whole].rearrange("(t p e) -> p t e", p=P, e=P)).then_inc(rows_in, 16)
                sp.dma_start(rows[0:k, CT - 1, :],
                             dram[whole:whole + k * P].rearrange("(p e) -> p e", e=P)).then_inc(rows_in, 16)
                sp.dma_start(rows[k:k + 1, CT - 1, 0:E - FULLCH * P],
                             dram[FULLCH * P:E].rearrange("(p e) -> p e", p=1)).then_inc(rows_in, 16)
            k = FULLG - GPT
            sp.dma_start(rowG[0:GPT, 0, :],
                         dst[0:GPT * GE].rearrange("(p e) -> p e", e=GE)).then_inc(rows_in, 16)
            sp.dma_start(rowG[0:k, 1, :],
                         dst[GPT * GE:FULLG * GE].rearrange("(p e) -> p e", e=GE)).then_inc(rows_in, 16)
            sp.dma_start(rowG[k:k + 1, 1, 0:GTAIL],
                         dst[FULLG * GE:E].rearrange("(p e) -> p e", p=1)).then_inc(rows_in, 16)
            sp.dma_start(lamB[:, :], lam.rearrange("(o c) -> o c", o=1).broadcast_to([P, 1])).then_inc(small_in, 16)
            sp.dma_start(condB[:, :], cond.rearrange("(o c) -> o c", o=1).broadcast_to([P, 2])).then_inc(small_in, 16)
            sp.wait_ge(xpad_ready, 1)
            sp.dma_start(x_nat[:, 0:HI - 1, :],
                         x[0:(HI - 1) * P, :].rearrange("(t p) f -> p t f", p=P)).then_inc(x_in, 16)
            sp.dma_start(x_nat[0:N - (HI - 1) * P, HI - 1, :], x[(HI - 1) * P:N, :]).then_inc(x_in, 16)

            def load_group(g, r, partitions=P):
                sp.dma_start(ebuf[0:partitions, r, :, 0:FE],
                             edge_attr[bass.ds(g * GE, partitions * GJ), :].rearrange("(p j) f -> p j f", j=GJ)
                             ).then_inc(e_in[r], 16)

            sp.wait_ge(const_ready, 2)
            for r in range(ERING):
                load_group(r, r)

            def store_block(mat, stage, i, c, staged, stored):
                sp.wait_ge(staged, (i * 2 + c + 1) * WPB + AHEAD)
                sp.dma_start(mat[bass.ds(i * 2 + c, 1), :, :].rearrange("o p n -> (o p) n"),
                             stage[c].rearrange("p s d -> p (s d)")).then_inc(stored[c], 16)

            def turn(i, partitions):
                for c in range(2):
                    for r in range(c * ERING // 2, (c + 1) * ERING // 2):
                        if partitions[r] is not None:
                            sp.wait_ge(e_used, i * ERING + r + 1)
                            g = 0 if partitions[r] == 0 else i * ERING + ERING + r
                            load_group(g, r, partitions[r] or P)
                    store_block(count_dram, stageC, i, c, count_out, count_stored)
                    store_block(wsum_dram, stageW, i, c, wsum_out, wsum_stored)

            with sp.Fori(0, NBODY - 2) as i:
                turn(i, [P] * ERING)
            last = (NBODY - 1) * ERING
            turn(NBODY - 2, [P if last + r < FULLG else GTAIL // GJ if last + r == FULLG else 0
                             for r in range(ERING)])
            turn(NBODY - 1, [None] * ERING)

            for c in range(2):
                sp.wait_ge(count_stored[c], 16 * NBODY)
                sp.wait_ge(wsum_stored[c], 16 * NBODY)
            sp.wait_ge(win_done, NWIN + AHEAD)
            sp.wait_ge(e_added, NG + AHEAD)

            def load_weights(k):
                sp.dma_start(unat, U_W[k, :, :]).then_inc(w_in, 16)
                sp.dma_start(ihnat, Wih[k, :, :].rearrange("(g a) b -> a g b", a=P)).then_inc(w_in, 16)
                sp.dma_start(hhnat, Whh[k, :, :].rearrange("(g a) b -> a g b", a=P)).then_inc(w_in, 16)
                sp.dma_start(bnat[:, 0:1], U_b[k, :].rearrange("(a o) -> a o", o=1)).then_inc(w_in, 16)
                sp.dma_start(bnat[:, 1:4], bih[k, :].rearrange("(g a) -> a g", a=P), allow_slow_non_contiguous=True).then_inc(w_in, 16)
                sp.dma_start(bnat[:, 4:7], bhh[k, :].rearrange("(g a) -> a g", a=P), allow_slow_non_contiguous=True).then_inc(w_in, 16)

            def load_half(mat, j, J, c):
                wait(sp, prod_done, J - 1)
                sp.dma_start(strm[c].rearrange("p b s d -> p b (s d)"),
                             mat[bass.ds(j * HB, HB), :, :].rearrange("b p n -> p b n")).then_inc(strm_in[c], 16)

            load_weights(0)
            for k in range(ROUNDS + 1):
                mat = count_dram if k < ROUNDS else wsum_dram
                for c in range(2):
                    load_half(mat, c, k * NHALF + c, c)
                if 0 < k < ROUNDS:
                    sp.wait_ge(h_ready, k * NHALF + AHEAD)
                    load_weights(k)
                with sp.Fori(1, NSUP) as i:
                    for c in range(2):
                        load_half(mat, i * 2 + c, i * 2 + (k * NHALF + c), c)

            for b in range(NTB):
                t0, n = batch(b)
                sp.wait_ge(res_ready, b + 1)
                if (t0 + n) * P <= N:
                    sp.dma_start(out[t0 * P:(t0 + n) * P, :].rearrange("(t p) f -> p t f", p=P),
                                 h_nat[:, t0:t0 + n, :]).then_inc(out_stored, 16)
                else:
                    sp.dma_start(out[t0 * P:N, :], h_nat[0:N - t0 * P, t0, :]).then_inc(out_stored, 16)
            sp.wait_ge(out_stored, 16 * NTB)

        @block.gpsimd
        def _(pool):
            def iota(out_ap, pattern, base=0, channel=0):
                return nc.gpsimd.iota(out_ap, pattern=pattern, base=base, channel_multiplier=channel,
                                      allow_small_or_imprecise_dtypes=True)

            nc.gpsimd.memset(x_nat[:, HI - 1, :], 0.0).then_inc(xpad_ready, 1)
            nc.gpsimd.memset(ident[:, :], 0.0).then_inc(const_ready, 1)
            nc.gpsimd.memset(ebuf[:, :, :, :], 1.0).then_inc(const_ready, 1)
            pool.wait_ge(const_ready, 1)
            nc.gpsimd.memset(ones[:, :], 1.0)
            nc.gpsimd.affine_select(out=ident[:, :], in_=ident[:, :], compare_op=ALU.not_equal, fill=1.0, base=0,
                                    pattern=[[-1, P]], channel_multiplier=1).then_inc(const_ready, 1)
            iota(iotaLo[:, :], [[1, P]])
            iota(iotaKey[:, :], [[1, WPB * KEYS]])
            iota(blkBase[:, :], [[WPB * KEYS, NBLK]])
            iota(iotaS[:, :], [[1, SW]])
            iota(further[:, :], [[-SW, N // SW + 1]], base=-SW)
            iota(winId[:, :], [[WPT, WT]], channel=1)
            nc.gpsimd.memset(sumE[:, :], 0.0)
            nc.gpsimd.memset(eaw[:, :], 0.0)
            nc.gpsimd.memset(zrow[:, :], 0.0).then_inc(const_ready, 1)
            pool.wait_ge(tab_turned, 6)
            iota(cLess, [[1, NCP]], base=-int(BIG))
            iota(cPlus, [[1, NCP]], base=1).then_inc(const_ready, 1)

            pool.wait_ge(tables_ready, 1)
            with pool.Fori(0, NBODY) as i:
                for u in range(2 * WPB):
                    w, s = i * (2 * WPB) + u, u % 2
                    c0 = pool.value_load(winTab[0:1, 0, bass.ds(w, 1)], min_val=0, max_val=NCH - 1)
                    pool.wait_ge(hot01_ready, w + 1)
                    nc.gpsimd.tensor_tensor(hot[s][3], hot[s][0], wT[2][:, bass.ds(c0, STEP)].rearrange(
                        "p (j o) -> p j o", o=1).broadcast_to([P, STEP, P]), ALU.mult).then_inc(hot3_ready, 1)

        @block.scalar
        def _(act):
            act.sem_inc(count_out, AHEAD)
            act.wait_ge(lam_ready, 2)
            act.wait_ge(rows_in, 15 * 16)
            nc.scalar.activation(rowW, rowDt, ACT.Exp, scale=lamN[:, 0:1]).then_inc(decay_ready, 1)

            for n, dest in enumerate((loT, keyT, wres)):
                for half in range(2):
                    cols = 512 if half == 0 else NCP - 512
                    act.wait_ge(tab_turned, 2 * n + half + 1)
                    nc.scalar.copy(dest[:, half * 512:half * 512 + cols],
                                   bank[2 * n + half][:, 0:cols]).then_inc(tab_out, 1)
            act.wait_ge(var_ready, 1)
            nc.scalar.activation(rstd[:, :], mv[:, :, 1], ACT.Sqrt).then_inc(std_ready, 1)
            for b in range(NTB):
                t0, n = batch(b)
                act.wait_ge(t_done, b + 1)
                nc.scalar.copy(hT[:, t0 * P:(t0 + n) * P], bank[6 + b % 2][:, 0:n * P]).then_inc(t_out, 1)

            act.wait_ge(tables_ready, 1)
            with act.Fori(0, NBODY) as i:
                for u in range(2 * WPB):
                    w, s, c = i * (2 * WPB) + u, u % 2, u // WPB
                    c0 = act.value_load(winTab[0:1, 0, bass.ds(w, 1)], min_val=0, max_val=NCH - 1)
                    act.wait_ge(hot01_ready, w + 1)
                    for j in range(STEP):
                        last = nc.scalar.activation(hot[s][2][:, j, :], hot[s][0][:, j, :], ACT.Copy,
                                                    scale=wT[1][:, bass.ds(c0 + j, 1)])
                    last.then_inc(hot2_ready, 1)
                    if u % WPB == 0:
                        with act.If(i > 0):
                            act.wait_ge(count_stored[c], i * 16)
                            act.sem_inc(count_stages, 1)
                    act.wait_ge(win_done, w + 1 + AHEAD)
                    d = u % WPB * WD
                    nc.scalar.copy(stageC[c][:, :, d:d + WD],
                                   psC[s][:, 0:KEYS].rearrange("p (d s) -> p s d", s=HI)).then_inc(count_out, 1)

            for j in range(NHALF):
                act.wait_ge(deg_spread, j + 1)
                nc.scalar.copy(degB[:, j * HALF:(j + 1) * HALF], bank[6 + j % 2][:, 0:HALF]).then_inc(deg_out, 1)

            def product_out(J, c):
                act.wait_ge(prod_done, J + 1)
                nc.scalar.copy(agg0[c][:, :], psP[c][:, 0:HALF]).then_inc(prod_out, 1)

            def message_out(J, c):
                act.wait_ge(msg_done, J + 1)
                nc.scalar.copy(agg[c][:, :], psM[:, 0:HALF]).then_inc(agg_ready, 1)

            def gates(J, c):
                act.wait_ge(gates_done, J + 1)
                nc.scalar.activation(gate[:, 0, :], psR[:, 0:HALF], ACT.Sigmoid, bias=brz[:, 0:1])
                nc.scalar.activation(gate[:, 1, :], psZ[:, 0:HALF], ACT.Sigmoid, bias=brz[:, 1:2]).then_inc(rz_ready, 1)
                act.wait_ge(cand_in, J + 1)
                nc.scalar.activation(gate[:, 2, :], gate[:, 3, :], ACT.Tanh, bias=bnat[:, 3:4]).then_inc(cand_ready, 1)

            for k in range(ROUNDS):
                for b in range(3):
                    act.wait_ge(w_turned, 3 * k + b + 1)
                    nc.scalar.copy(wts[:, 3 * b:3 * b + 3, :],
                                   bank[5 + b][:, 0:3 * F].rearrange("p (g c) -> p g c", g=3)).then_inc(w_ready, 1)
                J = k * NHALF
                product_out(J, 0)
                product_out(J + 1, 1)
                message_out(J, 0)
                with act.Fori(1, NSUP) as i:
                    for c in range(2):
                        product_out(i * 2 + (J + c), c)
                        message_out(i * 2 + (J + c - 1), 1 - c)
                        gates(i * 2 + (J + c - 2), c)
                J += NHALF
                message_out(J - 1, 1)
                gates(J - 2, 0)
                gates(J - 1, 1)
                if k < ROUNDS - 1:
                    for b in range(NTB):
                        t0, n = batch(b)
                        act.wait_ge(t_done, NTB * (k + 1) + b + 1)
                        nc.scalar.copy(h_nat[:, t0:t0 + n, :],
                                       bank[6 + b % 2][:, 0:n * P].rearrange("p (t f) -> p t f", f=F)).then_inc(t_out, 1)
            act.wait_ge(var_ready, 2)
            nc.scalar.activation(rstd[:, :], mv[:, :, 1], ACT.Sqrt).then_inc(std_ready, 1)
            with act.Fori(0, NSUP) as i:
                for c in range(2):
                    act.wait_ge(prod_done, i * 2 + (ROUNDS * NHALF + c + 1))
                    nc.scalar.copy(hT[:, bass.ds(i * (2 * HALF) + c * HALF, HALF)], psP[c][:, 0:HALF]).then_inc(prod_out, 1)

        @block.vector
        def _(dve):
            steps = [0]

            def link(ins):
                steps[0] += 1
                ins.then_inc(step_done, 1)
                dve.wait_ge(step_done, steps[0])

            dve.sem_inc(wsum_out, AHEAD)
            dve.sem_inc(e_added, AHEAD)
            dve.sem_inc(ex_added, AHEAD)
            dve.sem_inc(h_ready, AHEAD)
            nc.vector.memset(rowDst, NODST)
            nc.vector.memset(rowSrc, 0)
            nc.vector.memset(rowG, NODST).then_inc(pad_ready, 1)
            nc.vector.memset(rowDt, 0.0)
            nc.vector.memset(rowNorm, 0.0).then_inc(pad_ready, 1)
            dve.wait_ge(small_in, 32)
            nc.vector.tensor_scalar(lamN[:, :], lamB[:, :], 0.0, 1e-4, ALU.max, ALU.add).then_inc(lam_ready, 1)
            dve.wait_ge(lam_ready, 1)
            nc.vector.tensor_scalar(lamN[:, :], lamN[:, :], -1.0, None, ALU.mult).then_inc(lam_ready, 1)

            dve.wait_ge(rows_in, 15 * 16)
            nc.vector.tensor_reduce(chMM[:, 0, :], rowDst, AX.X, ALU.min)
            nc.vector.tensor_reduce(chMM[:, 1, :], rowDst, AX.X, ALU.max)
            nc.vector.tensor_reduce(gMM[0:GPT, 0, :], rowG[0:GPT], AX.X, ALU.min)
            nc.vector.tensor_reduce(gMM[0:GPT, 1, :], rowG[0:GPT], AX.X, ALU.max)
            nc.vector.tensor_copy(rowGf[0:GPT], rowG[0:GPT])
            nc.vector.tensor_single_scalar(rowHi, rowSrc, 7, ALU.arith_shift_right)
            link(nc.vector.tensor_single_scalar(rowLoI, rowSrc, P - 1, ALU.bitwise_and))
            nc.vector.tensor_copy(rowLo, rowLoI)
            nc.vector.scalar_tensor_tensor(rowKey, rowDst, float(HI), rowHi, ALU.mult, ALU.add)
            nc.vector.tensor_single_scalar(chMM[:, :, :], chMM[:, :, :], 3, ALU.arith_shift_right)
            nc.vector.tensor_scalar(gMMf[0:GPT], gMM[0:GPT], float(N - 1), None, ALU.min)
            dve.wait_ge(decay_ready, 1)
            link(nc.vector.tensor_tensor(rowW, rowW, rowNorm, ALU.mult))
            nc.vector.tensor_copy(chMMf[:, :, :], chMM[:, :, :]).then_inc(rows_ready, 1)
            dve.wait_ge(rows_ready, 1)

            dve.wait_ge(const_ready, 3)
            for k in range(2):
                for t in range(CT):
                    n = k * CT + t
                    wait(dve, diag_spread, n - 1)
                    nc.vector.tensor_scalar(diag[:, n % 2, :], ident[:, :], chMMf[:, k, t:t + 1], None,
                                            ALU.mult).then_inc(diag_ready, 1)
            for t in range(GT):
                n = 2 * CT + t
                dve.wait_ge(diag_spread, n - 1)
                nc.vector.tensor_scalar(diag[0:GPT, n % 2, 0:GPT], ident[0:GPT, 0:GPT], gMMf[0:GPT, 0, t:t + 1], None,
                                        ALU.mult).then_inc(diag_ready, 1)
            dve.wait_ge(tab_turned, 6)
            for k, dest in enumerate((chMinB, chMaxB)):
                dve.wait_ge(diag_spread, CT * (k + 1))
                nc.vector.tensor_copy(dest[:, 0:512], bank[2 * k][:, :])
                nc.vector.tensor_copy(dest[:, 512:NCP], bank[2 * k + 1][:, 0:NCP - 512]).then_inc(spread_out, 1)
            dve.wait_ge(spread_out, 2)
            dve.wait_ge(const_ready, 5)
            W = slice(0, WPT)
            for q in range(WT):
                link(nc.vector.tensor_scalar(m0[W], chMinB[W], winId[W, q:q + 1], None, ALU.is_le))
                link(nc.vector.scalar_tensor_tensor(m1[W], chMaxB[W], winId[W, q:q + 1], m0[W], ALU.is_ge, ALU.mult))
                link(nc.vector.tensor_tensor(m0[W], m1[W], cLess[W], ALU.mult))
                nc.vector.tensor_reduce(loHi[W, 0, q:q + 1], m0[W], AX.X, ALU.min)
                link(nc.vector.tensor_tensor(m1[W], m1[W], cPlus[W], ALU.mult))
                link(nc.vector.tensor_reduce(loHi[W, 1, q:q + 1], m1[W], AX.X, ALU.max))
            nc.vector.tensor_copy(cbv[:, 3:4], winId[:, 0:1]).then_inc(lohi_ready, 1)

            dve.wait_ge(grp_turned, 1)
            link(nc.vector.tensor_copy(dstG[:, :, 0], bank[4][:, 0:NG]))
            for j in range(GJ - 1, -1, -1):
                nc.vector.tensor_tensor(dstG[:, :, j], bank[5 + j // 2][:, (j % 2) * NG:(j % 2 + 1) * NG],
                                        dstG[:, :, 0], ALU.subtract)

            dve.wait_ge(lohi_turned, 1)
            dve.wait_ge(const_ready, 4)
            R = [rowTab[:, n, :] for n in range(4)]
            link(nc.vector.tensor_scalar(R[0], bank[0][0:1, 0:NWIN], BIG, float(NCH - 1), ALU.add, ALU.min))
            link(nc.vector.tensor_tensor(R[1], bank[1][0:1, 0:NWIN], R[0], ALU.subtract))
            link(nc.vector.tensor_scalar(R[1], R[1], -float(STEP), 0.0, ALU.add, ALU.max))
            link(nc.vector.tensor_tensor_scan(R[2], R[1], zrow[:, :], 0.0, ALU.add, ALU.add))
            link(nc.vector.tensor_tensor(R[2], R[2], R[1], ALU.subtract))
            link(nc.vector.tensor_copy(winTab[:, :, :], rowTab[:, 0:3, :]))
            G = [rowTab[:, n, 0:NG] for n in range(4)]
            nc.vector.tensor_copy(G[0], bank[2][0:1, 0:NG])
            link(nc.vector.tensor_copy(G[3], bank[2][0:1, NG:2 * NG]))
            link(nc.vector.tensor_tensor(G[1], G[3], G[0], ALU.subtract))
            link(nc.vector.tensor_copy(grpTab[:, 0:2, :], rowTab[:, 0:2, 0:NG]))
            link(nc.vector.tensor_single_scalar(grpTab[:, 1, :], grpTab[:, 1, :], 5, ALU.arith_shift_right))
            link(nc.vector.tensor_copy(G[1], grpTab[:, 1, :]))
            link(nc.vector.tensor_tensor_scan(G[2], G[1], zrow[:, 0:NG], 0.0, ALU.add, ALU.add))
            link(nc.vector.tensor_tensor(G[2], G[2], G[1], ALU.subtract))
            nc.vector.tensor_copy(grpTab[:, 2, :], G[2])

            dve.wait_ge(tab_out, 6)
            for q in range(3):
                link(nc.vector.tensor_copy(wbf, wres))
                link(nc.vector.tensor_copy(wT[q][:, :], wbf))
                if q < 2:
                    link(nc.vector.tensor_tensor(wres, wres, wT[q][:, :], ALU.subtract))

            def norm_stats():
                for t in range(HI):
                    last = nc.vector.bn_stats(stats[:, t, :], x_nat[:, t, :])
                link(last)
                for t in range(HI):
                    last = nc.vector.bn_aggr(mv[:, t, :], stats[:, t, :])
                link(last)
                nc.vector.tensor_scalar(mv[:, :, 1], mv[:, :, 1], EPS, None, ALU.add).then_inc(var_ready, 1)

            def norm_apply(n):
                dve.wait_ge(std_ready, n)
                link(nc.vector.reciprocal(rstd[:, :], rstd[:, :]))
                for t in range(HI):
                    last = nc.vector.tensor_scalar(h_nat[:, t, :], x_nat[:, t, :], mv[:, t, 0:1], rstd[:, t:t + 1],
                                                   ALU.subtract, ALU.mult)
                link(last)
                nc.vector.tensor_scalar(h_nat[:, :, :], h_nat[:, :, :], 0.0, None, ALU.max).then_inc(norm_ready, 1)

            dve.wait_ge(x_in, 32)
            norm_stats()
            norm_apply(1)
            dve.wait_ge(norm_ready, 1)
            nc.vector.tensor_copy(cbv[:, 3:4], winId[:, 0:1]).then_inc(tables_ready, 1)

            def window_hot(i, u):
                w, s, c, v = i * (2 * WPB) + u, u % 2, u // WPB, u % WPB
                c0 = dve.value_load(winTab[0:1, 0, bass.ds(w, 1)], min_val=0, max_val=NCH - 1)
                nx = dve.value_load(winTab[0:1, 1, bass.ds(w, 1)], min_val=0, max_val=NCH)
                xb = dve.value_load(winTab[0:1, 2, bass.ds(w, 1)], min_val=0, max_val=NCH * NWIN)
                blk = blkBase[:, bass.ds(i * 2 + c, 1)]
                keys = iotaKey[:, v * KEYS:(v + 1) * KEYS]
                dve.wait_ge(win_done, w - 1 + AHEAD)
                for j in range(STEP):
                    col = bass.ds(c0 + j, 1)
                    nc.vector.tensor_scalar(hot[s][0][:, j, :], iotaLo[:, :], loT[:, col], None, ALU.is_equal)
                    nc.vector.tensor_scalar(hot[s][1][:, j, :], iotaLo[:, :], loT[:, col], wT[0][:, col],
                                            ALU.is_equal, ALU.mult)
                    last = nc.vector.tensor_scalar(key[s][:, j, :], keys, blk, keyT[:, col], ALU.add, ALU.is_equal)
                last.then_inc(hot01_ready, 1)
                with dve.If(nx > 0):
                    with dve.Fori(0, nx) as n:
                        dve.wait_ge(xhot_used, xb + n + AHEAD)
                        col = bass.ds(nc.s_assert_within(c0 + STEP + n, 0, NCP - 1), 1)
                        nc.vector.tensor_scalar(xhot[0], iotaLo[:, :], loT[:, col], None, ALU.is_equal)
                        for q in range(3):
                            nc.vector.tensor_scalar(xhot[q + 1], iotaLo[:, :], loT[:, col], wT[q][:, col],
                                                    ALU.is_equal, ALU.mult)
                        nc.vector.tensor_scalar(xkey, keys, blk, keyT[:, col], ALU.add,
                                                ALU.is_equal).then_inc(xhot_ready, 1)

            def window_out(i, u):
                w, s, c = i * (2 * WPB) + u, u % 2, u // WPB
                if u % WPB == 0:
                    with dve.If(i > 0):
                        dve.wait_ge(wsum_stored[c], i * 16)
                        dve.sem_inc(wsum_stages, 1)
                dve.wait_ge(win_done, w + 1 + AHEAD)
                d = u % WPB * WD
                nc.vector.tensor_copy(stageW[c][:, :, d:d + WD],
                                      psW[s][:, 0:KEYS].rearrange("p (d s) -> p s d", s=HI)).then_inc(wsum_out, 1)

            def spread(t, n):
                return t.rearrange("p (o c) -> p o c", o=1).broadcast_to([P, GJ, n])

            def group_hot(i, r):
                g = i * ERING + r
                nx = dve.value_load(grpTab[0:1, 1, bass.ds(g, 1)], min_val=0, max_val=N // SW)
                xb = dve.value_load(grpTab[0:1, 2, bass.ds(g, 1)], min_val=0, max_val=NG * (N // SW))
                d0 = dve.value_load(grpTab[0:1, 0, bass.ds(g, 1)], min_val=0, max_val=N - 1)
                rel = dstG[:, bass.ds(g, 1), :].rearrange("p o j -> p (o j)")
                nc.vector.tensor_tensor(ehot[r % 2], spread(iotaS[:, :], SW),
                                        rel.rearrange("p (j o) -> p j o", o=1).broadcast_to([P, GJ, SW]),
                                        ALU.is_equal).then_inc(ehot_ready, 1)
                with dve.If(nx > 0):
                    with dve.Fori(0, nx) as n:
                        nc.vector.tensor_scalar(exrel, rel, further[:, bass.ds(n, 1)], None,
                                                ALU.add).then_inc(exrel_ready, 1)
                        dve.wait_ge(exrel_ready, xb + n + 1)
                        nc.vector.tensor_tensor(exhot, spread(iotaS[:, :], SW),
                                                exrel.rearrange("p (j o) -> p j o", o=1).broadcast_to([P, GJ, SW]),
                                                ALU.is_equal).then_inc(exhot_ready, 1)
                        dve.wait_ge(ex_done, xb + n + 1)
                        dve.wait_ge(e_added, g + AHEAD)
                        dve.wait_ge(ex_added, xb + n + AHEAD)
                        cols = bass.ds(nc.s_assert_within(d0 + n * SW + SW, 0, N - 1), SW)
                        nc.vector.tensor_tensor(sumE[:, cols], sumE[:, cols], psX[0:EA, 0:SW],
                                                ALU.add).then_inc(ex_added, 1)

            def group_add(i, r):
                g = i * ERING + r
                nx = dve.value_load(grpTab[0:1, 1, bass.ds(g, 1)], min_val=0, max_val=N // SW)
                xb = dve.value_load(grpTab[0:1, 2, bass.ds(g, 1)], min_val=0, max_val=NG * (N // SW))
                d0 = dve.value_load(grpTab[0:1, 0, bass.ds(g, 1)], min_val=0, max_val=N - 1)
                dve.wait_ge(e_used, g + 1)
                dve.wait_ge(e_added, g + AHEAD)
                dve.wait_ge(ex_added, xb + nx + AHEAD)
                cols = bass.ds(d0, SW)
                nc.vector.tensor_tensor(sumE[:, cols], sumE[:, cols], psE[r % 2][0:EA, 0:SW],
                                        ALU.add).then_inc(e_added, 1)

            with dve.Fori(0, NBODY) as i:
                for u in range(2 * WPB):
                    window_hot(i, u)
                    if u > 0:
                        window_out(i, u - 1)
                    if u % WPG == 0:
                        group_hot(i, u // WPG)
                    else:
                        group_add(i, u // WPG)
                window_out(i, 2 * WPB - 1)

            def weights(k):
                dve.wait_ge(w_in, 16 * 6 * (k + 1))
                nc.vector.tensor_copy(eaw[:, 0:FE], unat[:, 2 * F:2 * F + FE])
                nc.vector.tensor_tensor(brz[:, 0:2], bnat[:, 1:3], bnat[:, 4:6], ALU.add)
                link(nc.vector.scalar_tensor_tensor(cbv[:, 0:1], condB[:, 0:1], unat[:, 2 * F + FE:2 * F + FE + 1],
                                                    bnat[:, 0:1], ALU.mult, ALU.add))
                nc.vector.scalar_tensor_tensor(eaw[:, FE:FE + 1], condB[:, 1:2], unat[:, 2 * F + FE + 1:2 * F + FE + 2],
                                               cbv[:, 0:1], ALU.mult, ALU.add).then_inc(w_prep, 1)

            def times_degree(j, J, c):
                wait(dve, msg_done, J - 1)
                cols = bass.ds(j * HALF, HALF)
                nc.vector.tensor_tensor(hdeg[c][:, :], hT[:, cols], degB[:, cols], ALU.mult).then_inc(hdeg_ready, 1)

            def update(j, J):
                cols = bass.ds(j * HALF, HALF)
                dve.wait_ge(rz_ready, J + 1)
                nc.vector.scalar_tensor_tensor(gate[:, 3, :], psH[:, 0:HALF], bnat[:, 6:7], gate[:, 0, :],
                                               ALU.add, ALU.mult).then_inc(gru_step, 1)
                dve.wait_ge(gru_step, J * 3 + 1)
                nc.vector.tensor_tensor(gate[:, 3, :], gate[:, 3, :], psI[:, 0:HALF], ALU.add).then_inc(cand_in, 1)
                dve.wait_ge(cand_ready, J + 1)
                nc.vector.tensor_tensor(gate[:, 3, :], hT[:, cols], gate[:, 2, :], ALU.subtract).then_inc(gru_step, 1)
                dve.wait_ge(gru_step, J * 3 + 2)
                nc.vector.tensor_tensor(gate[:, 3, :], gate[:, 3, :], gate[:, 1, :], ALU.mult).then_inc(gru_step, 1)
                dve.wait_ge(gru_step, J * 3 + 3)
                nc.vector.tensor_tensor(hT[:, cols], gate[:, 2, :], gate[:, 3, :], ALU.add).then_inc(h_ready, 1)

            dve.wait_ge(deg_out, NHALF)
            for k in range(ROUNDS):
                weights(k)
                J = k * NHALF
                dve.wait_ge(h_ready, J + AHEAD)
                times_degree(0, J, 0)
                times_degree(1, J + 1, 1)
                with dve.Fori(1, NSUP) as i:
                    for c in range(2):
                        times_degree(i * 2 + c, i * 2 + (J + c), c)
                        update(i * 2 + (c - 2), i * 2 + (J + c - 2))
                J += NHALF
                update(NHALF - 2, J - 2)
                update(NHALF - 1, J - 1)

            for b in range(NTB):
                t0, n = batch(b)
                dve.wait_ge(t_done, NTB * (ROUNDS + 0) + b + 1)
                last = nc.vector.tensor_tensor(x_nat[:, t0:t0 + n, :], x_nat[:, t0:t0 + n, :],
                                               bank[6 + b % 2][:, 0:n * P].rearrange("p (t f) -> p t f", f=F),
                                               ALU.add).then_inc(t_out, 1)
            dve.wait_ge(t_out, NTB * (ROUNDS + 1))
            norm_stats()
            norm_apply(2)
            for b in range(NTB):
                t0, n = batch(b)
                dve.wait_ge(t_done, NTB * (ROUNDS + 1) + b + 1)
                nc.vector.tensor_tensor(h_nat[:, t0:t0 + n, :], x_nat[:, t0:t0 + n, :],
                                        bank[6 + b % 2][:, 0:n * P].rearrange("p (t f) -> p t f", f=F),
                                        ALU.add).then_inc(res_ready, 1)

        @block.tensor
        def _(pe):
            pe.sem_inc(win_done, AHEAD)
            pe.sem_inc(xhot_used, AHEAD)
            pe.wait_ge(const_ready, 3)
            pe.wait_ge(rows_ready, 1)
            for n, rows in enumerate((rowLo, rowKey, rowW)):
                for t in range(CT):
                    last = nc.tensor.transpose(bank[2 * n + t // 4][:, t % 4 * P:(t % 4 + 1) * P], rows[:, t, :],
                                               ident[:, :])
                    if t == 3 or t == CT - 1:
                        last.then_inc(tab_turned, 1)
            for k in range(2):
                pe.wait_ge(tab_out, 2 * (k + 1))
                for t in range(CT):
                    n = k * CT + t
                    pe.wait_ge(diag_ready, n + 1)
                    nc.tensor.matmul(bank[2 * k + t // 4][:, t % 4 * P:(t % 4 + 1) * P], ones[:, :],
                                     diag[:, n % 2, :], start=True, stop=True).then_inc(diag_spread, 1)
            pe.wait_ge(tab_out, 6)
            for t in range(GT):
                pe.wait_ge(diag_ready, 2 * CT + t + 1)
                nc.tensor.matmul(bank[4][:, t * GPT:(t + 1) * GPT], ones[0:GPT, :],
                                 diag[0:GPT, (2 * CT + t) % 2, 0:GPT], start=True, stop=True).then_inc(diag_spread, 1)
            for j in range(GJ):
                for t in range(GT):
                    last = nc.tensor.transpose(bank[5 + j // 2][:, (j % 2) * NG + t * GPT:(j % 2) * NG + (t + 1) * GPT],
                                               rowGf[0:GPT, t, bass.ds(j, P, GJ)], ident[0:GPT, 0:GPT])
            last.then_inc(grp_turned, 1)
            pe.wait_ge(lohi_ready, 1)
            for k in range(2):
                for q in range(WT):
                    nc.tensor.matmul(bank[k][0:1, q * WPT:(q + 1) * WPT], loHi[0:WPT, k, q:q + 1],
                                     ident[0:WPT, 0:WPT], start=True, stop=True)
                for t in range(GT):
                    last = nc.tensor.matmul(bank[2][0:1, k * NG + t * GPT:k * NG + (t + 1) * GPT],
                                            gMMf[0:GPT, k, t:t + 1], ident[0:GPT, 0:GPT], start=True, stop=True)
            last.then_inc(lohi_turned, 1)

            def turn_tiles(source, n0):
                for b in range(NTB):
                    t0, n = batch(b)
                    if b >= 2:
                        pe.wait_ge(res_ready if n0 > NTB * ROUNDS else t_out,
                                   b - 1 if n0 > NTB * ROUNDS else n0 + b - 1)
                    for t in range(n):
                        last = nc.tensor.transpose(bank[6 + b % 2][:, t * P:(t + 1) * P], source(t0 + t), ident[:, :])
                    last.then_inc(t_done, 1)

            pe.wait_ge(norm_ready, 1)
            turn_tiles(lambda t: h_nat[:, t, :], 0)
            pe.wait_ge(tables_ready, 1)
            pe.wait_ge(t_out, NTB)

            def window(i, u):
                w, s = i * (2 * WPB) + u, u % 2
                nx = pe.value_load(winTab[0:1, 1, bass.ds(w, 1)], min_val=0, max_val=NCH)
                xb = pe.value_load(winTab[0:1, 2, bass.ds(w, 1)], min_val=0, max_val=NCH * NWIN)
                pe.wait_ge(hot01_ready, w + 1)
                pe.wait_ge(hot2_ready, w + 1)
                pe.wait_ge(hot3_ready, w + 1)
                pe.wait_ge(count_out, w - 1 + AHEAD)
                pe.wait_ge(wsum_out, w - 1 + AHEAD)

                def chunk(rows, keys, first, final):
                    nc.tensor.matmul(psC[s][:, 0:KEYS], rows[0], keys, start=first, stop=final)
                    for q in range(3):
                        last = nc.tensor.matmul(psW[s][:, 0:KEYS], rows[q + 1], keys, start=first and q == 0,
                                                stop=final and q == 2)
                    return last

                chunk([hot[s][q][:, 0, :] for q in range(4)], key[s][:, 0, :], True, False)
                with pe.If(nx > 0):
                    with pe.Fori(0, nx) as n:
                        pe.wait_ge(xhot_ready, xb + n + 1)
                        chunk(xhot, xkey, False, False).then_inc(xhot_used, 1)
                for j in range(1, STEP):
                    last = chunk([hot[s][q][:, j, :] for q in range(4)], key[s][:, j, :], False, j == STEP - 1)
                last.then_inc(win_done, 1)

            def group(i, r):
                g = i * ERING + r
                nx = pe.value_load(grpTab[0:1, 1, bass.ds(g, 1)], min_val=0, max_val=N // SW)
                xb = pe.value_load(grpTab[0:1, 2, bass.ds(g, 1)], min_val=0, max_val=NG * (N // SW))
                pe.wait_ge(e_in[r], i * 16 + 16)
                pe.wait_ge(ehot_ready, g + 1)
                with pe.If(nx > 0):
                    with pe.Fori(0, nx) as n:
                        pe.wait_ge(exhot_ready, xb + n + 1)
                        for j in range(GJ):
                            last = nc.tensor.matmul(psX[0:EA, 0:SW], ebuf[:, r, j, :], exhot[:, j, :],
                                                    start=j == 0, stop=j == GJ - 1)
                        last.then_inc(ex_done, 1)
                pe.wait_ge(e_added, g - 1 + AHEAD)
                for j in range(GJ):
                    last = nc.tensor.matmul(psE[r % 2][0:EA, 0:SW], ebuf[:, r, j, :], ehot[r % 2][:, j, :],
                                            start=j == 0, stop=j == GJ - 1)
                last.then_inc(e_used, 1)

            with pe.Fori(0, NBODY) as i:
                for u in range(2 * WPB):
                    window(i, u)
                    if u % WPG == 0:
                        group(i, u // WPG)

            pe.wait_ge(e_added, NG + AHEAD)
            for j in range(NHALF):
                if j >= 2:
                    pe.wait_ge(deg_out, j - 1)
                nc.tensor.matmul(bank[6 + j % 2][:, 0:HALF], ones[FE:FE + 1, :],
                                 sumE[FE:FE + 1, j * HALF:(j + 1) * HALF], start=True, stop=True).then_inc(deg_spread, 1)
            pe.wait_ge(deg_out, NHALF)
            pe.wait_ge(count_out, NWIN + AHEAD)
            pe.wait_ge(wsum_out, NWIN + AHEAD)

            def product(J, c):
                pe.wait_ge(strm_in[c], 8 * (J - c) + 16)
                wait(pe, prod_out, J - 1)
                for s in range(HI):
                    last = nc.tensor.matmul(psP[c][:, 0:HALF], h_nat[:, s, :], strm[c][:, :, s, :],
                                            start=s == 0, stop=s == HI - 1)
                last.then_inc(prod_done, 1)

            def message(j, J, c):
                pe.wait_ge(prod_out, J + 1)
                pe.wait_ge(hdeg_ready, J + 1)
                wait(pe, agg_ready, J)
                nc.tensor.matmul(psM[:, 0:HALF], wts[:, 1, :], agg0[c][:, :], start=True, stop=False)
                nc.tensor.matmul(psM[:, 0:HALF], wts[:, 0, :], hdeg[c][:, :], start=False, stop=False)
                nc.tensor.matmul(psM[:, 0:HALF], wts[0:EA, 2, :], sumE[0:EA, bass.ds(j * HALF, HALF)],
                                 start=False, stop=True).then_inc(msg_done, 1)

            def gru(j, J, c):
                pe.wait_ge(agg_ready, J + 1)
                pe.wait_ge(h_ready, J + AHEAD)
                cols = bass.ds(j * HALF, HALF)
                for g, ps in ((0, psR), (1, psZ)):
                    nc.tensor.matmul(ps[:, 0:HALF], wts[:, 3 + g, :], agg[c][:, :], start=True, stop=False)
                    nc.tensor.matmul(ps[:, 0:HALF], wts[:, 6 + g, :], hT[:, cols], start=False, stop=True)
                nc.tensor.matmul(psI[:, 0:HALF], wts[:, 5, :], agg[c][:, :], start=True, stop=True)
                nc.tensor.matmul(psH[:, 0:HALF], wts[:, 8, :], hT[:, cols], start=True, stop=True).then_inc(gates_done, 1)

            for k in range(ROUNDS):
                pe.wait_ge(w_prep, k + 1)
                wait(pe, t_out, NTB * (k + 1))
                pe.wait_ge(h_ready, k * NHALF + AHEAD)
                raw = [unat[:, 0:F], unat[:, F:2 * F], eaw[:, :]] + [ihnat[:, g, :] for g in range(3)] + \
                      [hhnat[:, g, :] for g in range(3)]
                for n, m in enumerate(raw):
                    last = nc.tensor.transpose(bank[5 + n // 3][:, n % 3 * F:(n % 3 + 1) * F], m, ident[:, :])
                    if n % 3 == 2:
                        last.then_inc(w_turned, 1)
                J = k * NHALF
                product(J, 0)
                product(J + 1, 1)
                pe.wait_ge(w_ready, 3 * (k + 1))
                message(0, J, 0)
                with pe.Fori(1, NSUP) as i:
                    for c in range(2):
                        product(i * 2 + (J + c), c)
                        message(i * 2 + (c - 1), i * 2 + (J + c - 1), 1 - c)
                        gru(i * 2 + (c - 2), i * 2 + (J + c - 2), c)
                J += NHALF
                message(NHALF - 1, J - 1, 1)
                gru(NHALF - 2, J - 2, 0)
                gru(NHALF - 1, J - 1, 1)
                pe.wait_ge(h_ready, J + AHEAD)
                turn_tiles(lambda t: hT[:, t * P:(t + 1) * P], NTB * (k + 1))

            pe.wait_ge(norm_ready, 2)
            J = ROUNDS * NHALF
            with pe.Fori(0, NSUP) as i:
                for c in range(2):
                    product(i * 2 + (J + c), c)
            pe.wait_ge(prod_out, J + NHALF)
            turn_tiles(lambda t: hT[:, t * P:(t + 1) * P], NTB * (ROUNDS + 1))

    return nc


_ORDER = ["x", "src", "dst", "edge_attr_64", "edge_weight", "edge_weight_n2", "L0_gnn_cond", "L0_gnn_U_W", "L0_gnn_U_b",
          "L0_gnn_Wih", "L0_gnn_Whh", "L0_gnn_bih", "L0_gnn_bhh", "L1_gnn_decay_lam"]


def kernel(**inputs):
    import numpy as np
    import concourse.bacc as bacc
    from concourse.bass_utils import run_bass_kernel_spmd

    nc = bacc.Bacc("TRN2", target_bir_lowering=False, num_devices=1)
    arrays, args = {}, []
    for name in _ORDER:
        a = np.ascontiguousarray(inputs[name])
        arrays[f"in_{name}"] = a
        args.append(nc.dram_tensor(f"in_{name}", a.shape, mybir.dt.from_np(a.dtype), kind="ExternalInput").ap())
    out = nc.dram_tensor("out", (N, F), mybir.dt.float32, kind="ExternalOutput").ap()
    build(nc, *args, out)
    r = run_bass_kernel_spmd(nc, [arrays], core_ids=[0])
    return r.results[0]["out"]
```

```python
import concourse.bass as bass
from concourse import mybir
from contextlib import ExitStack

N, E, F, FE = 3125, 100000, 128, 64
ROUNDS = 3
P = 128
HI = -(-N // P)
NP = HI * P
WD = 7
KEYS = WD * HI
WPB = 8
BD = WPB * WD
BCOLS = HI * BD
NBLK = -(-N // BD)
ND = NBLK * BD
NWIN = NBLK * WPB
QUAD = 4
NQ = NWIN // QUAD
STEP = 2
TAKE = STEP * P
WT = 4
WPT = NWIN // WT
NCH = -(-E // P)
CT = -(-NCH // P)
NCP = CT * P
FULLCH = E // P
REC = 5
NODST = 4095
BIG = 1024.0
NBODY = NBLK // 2
WPTURN = 2 * WPB
QPB = WPTURN // QUAD
GE = 512
GJ = GE // P
ERING = 7
NG = NBODY * ERING
GT = 2
GPT = NG // GT
FULLG = E // GE
GTAIL = E - FULLG * GE
SW = 32
EA = FE + 1
HB = 7
HALF = HB * BD
NHALF = NBLK // HB
NSUP = NHALF // 2
EPS = 1e-5
assert NG == FULLG + 1 and TAKE >= KEYS


def build(nc, x, src, dst, edge_attr, dt_in, norm_in, cond, U_W, U_b, Wih, Whh, bih, bhh, lam, out):
    f32, bf16, i32 = mybir.dt.float32, mybir.dt.bfloat16, mybir.dt.int32
    f16 = mybir.dt.float16
    ALU, ACT, AX = mybir.AluOpType, mybir.ActivationFunctionType, mybir.AxisListType

    ctx = ExitStack()
    with ctx:
        def sb(name, shape, dt=f32):
            return ctx.enter_context(nc.sbuf_tensor(name, shape, dt))

        def pb(name, shape):
            return ctx.enter_context(nc.psum_tensor(name, shape, f32))

        def sem(name):
            return ctx.enter_context(nc.semaphore(name))

        mat_dram = nc.dram_tensor("mat_dram", [NBLK, 2, P, BCOLS], f32, kind="Internal").ap()
        rec_dram = nc.dram_tensor("rec_dram", [NCP * P, REC], f32, kind="Internal").ap()
        dst_dram = nc.dram_tensor("dst_dram", [NCP, P], i32, kind="Internal").ap()

        ident = sb("ident", [P, P])
        ones = sb("ones", [P, P])
        x_nat = sb("x_nat", [P, HI, F])
        h_nat = sb("h_nat", [P, HI, F])
        hT = sb("hT", [P, NP])
        degB = sb("degB", [P, ND])
        sumE = sb("sumE", [EA, ND + SW])
        stats = sb("stats", [P, HI, 6])
        mv = sb("mv", [P, HI, 2])
        rstd = sb("rstd", [P, HI])

        startTab = sb("startTab", [1, NWIN], i32)
        furtherTab = sb("furtherTab", [1, NWIN], i32)
        beforeTab = sb("beforeTab", [1, NWIN], i32)
        quadTab = sb("quadTab", [1, NQ], i32)
        grpFirst = sb("grpFirst", [1, NBODY, 8], i32)
        grpFurther = sb("grpFurther", [1, NG], i32)
        grpBefore = sb("grpBefore", [1, NG], i32)
        turnTab = sb("turnTab", [1, NBODY], i32)
        iotaLo = sb("iotaLo", [P, P], f16)
        iotaKey = sb("iotaKey", [P, KEYS], f16)
        winBase = sb("winBase", [P, NWIN])
        iotaS = sb("iotaS", [P, SW])
        further = sb("further", [P, N // SW + 1])
        dstG = sb("dstG", [P, NG, GJ])

        AREA = 2 * HB * BCOLS
        area = sb("area", [P, AREA])

        def carve(at, cols, dt=f32):
            v = area[:, at:at + cols]
            return v if dt == f32 else v.bitcast(dt)

        ROW = CT * P

        def take_rows(at, dt=f32, t=CT, e=P):
            return carve(at, t * e, dt).rearrange("p (t e) -> p t e", t=t)
        rowDst, rowSrc, rowHi, rowLoI = (take_rows(n * ROW, i32) for n in range(4))
        rowDt, rowNorm, rowW = (take_rows(n * ROW) for n in range(4, 7))
        rowRec = carve(7 * ROW, ROW * REC).rearrange("p (t e f) -> p t e f", t=CT, f=REC)
        rowG = take_rows(12 * ROW, i32, GT, GE)
        rowGf = take_rows(12 * ROW + GT * GE, f32, GT, GE)
        a0 = 12 * ROW + 2 * GT * GE
        wbf = [carve(a0 + q * ROW // 2, ROW // 2, bf16).rearrange("p (t e) -> p t e", t=CT) for q in range(3)]
        a0 += 3 * ROW // 2
        diag = carve(a0, 2 * P).rearrange("p (k c) -> p k c", k=2)
        gath = carve(a0 + 2 * P, 2 * WT * P, i32).rearrange("p (k q e) -> p k q e", k=2, q=WT)
        rel = carve(a0 + 2 * P + 2 * WT * P, 2 * WT * P).rearrange("p (k q e) -> p k q e", k=2, q=WT)
        assert a0 + 2 * P + 4 * WT * P <= AREA
        chMinB, chMaxB, m0 = (degB[:, n * NCP:(n + 1) * NCP] for n in range(3))
        m1 = sb("m1", [P, NCP])
        cLess = sb("cLess", [P, NCP])
        cPlus = sb("cPlus", [P, NCP])
        chMM = sb("chMM", [P, 2, CT])
        gMM = sb("gMM", [P, 2, GT])
        winLo = sb("winLo", [P, WT])
        winHi = sb("winHi", [P, WT])
        loHi = sb("loHi", [P, 2, WT])
        rowIdx = sb("rowIdx", [P, 2, WT], i32)
        posLH = sb("posLH", [P, 2, WT])
        colTab = sb("colTab", [P, 2, WT])
        colInt = sb("colInt", [P, WT], i32)
        rowTab = sb("rowTab", [1, 4, NWIN])
        zrow = sb("zrow", [1, NWIN])
        lamB = sb("lamB", [P, 1])
        lamN = sb("lamN", [P, 1])
        condB = sb("condB", [P, 2])
        mscale = sb("mscale", [P, HI])

        at = 0

        def take(cols, dt=f32):
            nonlocal at
            v = carve(at, cols, dt)
            at += cols
            return v
        hot = [[take(STEP * P // 2, bf16).rearrange("p (j c) -> p j c", j=STEP) for _ in range(4)] for _ in range(2)]
        KP = KEYS + 1
        key = [take(STEP * KP // 2, bf16).rearrange("p (j c) -> p j c", j=STEP) for _ in range(2)]
        xhot = [take(P // 2, bf16) for _ in range(4)]
        xkey = take(KP // 2, bf16)
        stage = [take(2 * BCOLS).rearrange("p (m s d) -> p m s d", m=2, s=HI) for _ in range(2)]
        ehot = [take(GJ * SW).rearrange("p (j c) -> p j c", j=GJ) for _ in range(ERING)]
        exhot = take(GJ * SW).rearrange("p (j c) -> p j c", j=GJ)
        exrel = take(GJ)
        recs = take(WPTURN * STEP * REC).rearrange("p (w j f) -> p w j f", w=WPTURN, j=STEP)
        keyrel = take(WPTURN * STEP).rearrange("p (w j) -> p w j", w=WPTURN)
        xrec = take(REC)
        xkeyrel = take(1)
        assert at <= AREA
        ebuf = sb("ebuf", [P, ERING, GJ, EA])

        at = 0
        strm = [take(HB * BCOLS).rearrange("p (b s d) -> p b s d", b=HB, s=HI) for _ in range(2)]
        assert at <= AREA
        agg0 = [sb(f"agg0{c}", [P, HALF]) for c in range(2)]
        hdeg = [sb(f"hdeg{c}", [P, HALF]) for c in range(2)]
        agg = [sb(f"agg{c}", [P, HALF]) for c in range(2)]
        gate = sb("gate", [P, 4, HALF])
        wnat = ebuf[:, :, :, :].rearrange("p a b c -> p (a b c)")
        unat = wnat[:, 0:2 * F + FE + 2]
        ihnat = wnat[:, 384:384 + 3 * F].rearrange("p (g c) -> p g c", g=3)
        hhnat = wnat[:, 768:768 + 3 * F].rearrange("p (g c) -> p g c", g=3)
        cbv = sb("cbv", [P, 4])
        bnat = sb("bnat", [P, 7])
        brz = sb("brz", [P, 2])
        eaw = sb("eaw", [P, F])
        wts = sb("wts", [P, 9, F])

        bank = [pb(f"bank{i}", [P, 512]) for i in range(8)]
        psC, psW, psE, psXC, psXW = bank[0:2], bank[2:4], bank[4:6], bank[6], bank[7]
        psP, psM, psR, psZ, psI, psH, psT = bank[0:2], bank[2], bank[3], bank[4], bank[5], bank[6], bank[7]

        const_ready = sem("const_ready")
        pad_ready = sem("pad_ready")
        rows_in = sem("rows_in")
        small_in = sem("small_in")
        xpad_ready = sem("xpad_ready")
        x_in = sem("x_in")
        lam_ready = sem("lam_ready")
        decay_ready = sem("decay_ready")
        int_ready = sem("int_ready")
        part_ready = sem("part_ready")
        extremes_ready = sem("extremes_ready")
        key_ready = sem("key_ready")
        recs_ready = sem("recs_ready")
        dst_stored = sem("dst_stored")
        rec_stored = sem("rec_stored")
        idx_ready = sem("idx_ready")
        gathered = sem("gathered")
        scale_ready = sem("scale_ready")
        step_done = sem("step_done")
        diag_ready = sem("diag_ready")
        diag_spread = sem("diag_spread")
        spread_out = sem("spread_out")
        lohi_ready = sem("lohi_ready")
        grp_turned = sem("grp_turned")
        lohi_turned = sem("lohi_turned")
        tables_ready = sem("tables_ready")
        var_ready = sem("var_ready")
        std_ready = sem("std_ready")
        norm_ready = sem("norm_ready")
        e_in = [sem(f"e_in{r}") for r in range(ERING)]
        ehot_ready = sem("ehot_ready")
        e_used = sem("e_used")
        e_added = sem("e_added")
        exrel_ready = sem("exrel_ready")
        exhot_ready = sem("exhot_ready")
        ex_done = sem("ex_done")
        ex_added = sem("ex_added")
        hot0_ready = sem("hot0_ready")
        hot1_ready = sem("hot1_ready")
        hot2_ready = sem("hot2_ready")
        hot3_ready = sem("hot3_ready")
        win_done = sem("win_done")
        xhot_ready = sem("xhot_ready")
        xhot_used = sem("xhot_used")
        xrec_in = sem("xrec_in")
        xkeyrel_ready = sem("xkeyrel_ready")
        x_added = sem("x_added")
        rec_in = [sem(f"rec_in{k}") for k in range(QPB)]
        keyrel_ready = sem("keyrel_ready")
        stored = [sem(f"stored{c}") for c in range(2)]
        stages = sem("stages")
        win_out = sem("win_out")
        block_ready = sem("block_ready")
        deg_spread = sem("deg_spread")
        deg_out = sem("deg_out")
        strm_in = [sem(f"strm_in{c}") for c in range(2)]
        prod_done = sem("prod_done")
        prod_out = sem("prod_out")
        hdeg_ready = sem("hdeg_ready")
        msg_done = sem("msg_done")
        agg_ready = sem("agg_ready")
        gates_done = sem("gates_done")
        rz_ready = sem("rz_ready")
        cand_in = sem("cand_in")
        cand_ready = sem("cand_ready")
        gru_step = sem("gru_step")
        h_ready = sem("h_ready")
        w_in = sem("w_in")
        w_prep = sem("w_prep")
        w_turned = sem("w_turned")
        w_ready = sem("w_ready")
        t_done = sem("t_done")
        t_out = sem("t_out")
        res_ready = sem("res_ready")
        out_stored = sem("out_stored")

        AHEAD = 2
        NTB = -(-HI // 4)

        def batch(b):
            return 4 * b, min(4, HI - 4 * b)

        def wait(eng, s, v):
            if not (isinstance(v, int) and v <= 0):
                eng.wait_ge(s, v)

        def entry_regs(eng, name):
            return [eng.alloc_register(f"{name}_entry{n}") for n in range(QUAD)]

        def read4(eng, regs, row, most):
            eng.load(regs, row)
            return [eng.snap(g, min_val=0, max_val=most) for g in regs]

        block = ctx.enter_context(nc.Block())

        @block.sync
        def _(sp):
            sp.wait_ge(pad_ready, 2)
            whole = (CT - 1) * P * P
            k = FULLCH - (CT - 1) * P
            for rows, dram in ((rowDst, dst), (rowSrc, src), (rowDt, dt_in), (rowNorm, norm_in)):
                sp.dma_start(rows[:, 0:CT - 1, :],
                             dram[0:whole].rearrange("(t p e) -> p t e", p=P, e=P)).then_inc(rows_in, 16)
                sp.dma_start(rows[0:k, CT - 1, :],
                             dram[whole:whole + k * P].rearrange("(p e) -> p e", e=P)).then_inc(rows_in, 16)
                sp.dma_start(rows[k:k + 1, CT - 1, 0:E - FULLCH * P],
                             dram[FULLCH * P:E].rearrange("(p e) -> p e", p=1)).then_inc(rows_in, 16)
            k = FULLG - GPT
            sp.dma_start(rowG[0:GPT, 0, :],
                         dst[0:GPT * GE].rearrange("(p e) -> p e", e=GE)).then_inc(rows_in, 16)
            sp.dma_start(rowG[0:k, 1, :],
                         dst[GPT * GE:FULLG * GE].rearrange("(p e) -> p e", e=GE)).then_inc(rows_in, 16)
            sp.dma_start(rowG[k:k + 1, 1, 0:GTAIL],
                         dst[FULLG * GE:E].rearrange("(p e) -> p e", p=1)).then_inc(rows_in, 16)
            sp.dma_start(lamB[:, :], lam.rearrange("(o c) -> o c", o=1).broadcast_to([P, 1])).then_inc(small_in, 16)
            sp.dma_start(condB[:, :], cond.rearrange("(o c) -> o c", o=1).broadcast_to([P, 2])).then_inc(small_in, 16)
            sp.wait_ge(xpad_ready, 1)
            sp.dma_start(x_nat[:, 0:HI - 1, :],
                         x[0:(HI - 1) * P, :].rearrange("(t p) f -> p t f", p=P)).then_inc(x_in, 16)
            sp.dma_start(x_nat[0:N - (HI - 1) * P, HI - 1, :], x[(HI - 1) * P:N, :]).then_inc(x_in, 16)
            sp.wait_ge(rows_in, 15 * 16)
            sp.dma_start(dst_dram.rearrange("(t p) e -> p t e", p=P), rowDst).then_inc(dst_stored, 16)

            def load_group(g, r, partitions=P):
                sp.dma_start(ebuf[0:partitions, r, :, 0:FE],
                             edge_attr[bass.ds(g * GE, partitions * GJ), :].rearrange("(p j) f -> p j f", j=GJ)
                             ).then_inc(e_in[r], 16)

            sp.wait_ge(const_ready, 2)
            for r in range(ERING):
                load_group(r, r)
            sp.wait_ge(recs_ready, 1)
            sp.dma_start(rec_dram.rearrange("(t p e) f -> p t (e f)", p=P, e=P),
                         rowRec.rearrange("p t e f -> p t (e f)")).then_inc(rec_stored, 16)

            regs = entry_regs(sp, "sp")

            def load_records(i, k):
                starts = read4(sp, regs, startTab[0:1, bass.ds(i * WPTURN + k * QUAD, QUAD)], E + 2 * P)
                for v in range(QUAD):
                    sp.dma_start(recs[:, k * QUAD + v, :, :].rearrange("p j f -> p (j f)"),
                                 rec_dram[bass.ds(starts[v], TAKE), :].rearrange("(p j) f -> p (j f)", j=STEP)
                                 ).then_inc(rec_in[k], 16)

            sp.wait_ge(rec_stored, 16)
            sp.wait_ge(tables_ready, 1)
            for k in range(QPB):
                load_records(0, k)

            def further_records(i, k):
                any_further = sp.value_load(quadTab[0:1, bass.ds(i * QPB + k, 1)], min_val=0, max_val=NCH * QUAD)
                with sp.If(any_further > 0):
                    for v in range(QUAD):
                        w = i * WPTURN + (k * QUAD + v)
                        nx = sp.value_load(furtherTab[0:1, bass.ds(w, 1)], min_val=0, max_val=NCH)
                        with sp.If(nx > 0):
                            xb = sp.value_load(beforeTab[0:1, bass.ds(w, 1)], min_val=0, max_val=NCH * NWIN)
                            e0 = sp.value_load(startTab[0:1, bass.ds(w, 1)], min_val=0, max_val=E)
                            with sp.Fori(0, nx) as n:
                                sp.wait_ge(xhot_used, xb + n + AHEAD)
                                at = nc.s_assert_within(e0 + n * P + TAKE, 0, NCP * P - P)
                                sp.dma_start(xrec, rec_dram[bass.ds(at, P), :]).then_inc(xrec_in, 16)

            def turn(i, partitions):
                for k in range(QPB):
                    further_records(i, k)
                    if partitions is None:
                        continue
                    for ready in (hot1_ready, hot2_ready, hot3_ready):
                        sp.wait_ge(ready, i * WPTURN + (k + 1) * QUAD)
                    load_records(i + 1, k)
                    for r in range(2 * k, min(2 * k + 2, ERING)):
                        sp.wait_ge(e_used, i * ERING + r + 1)
                        load_group(i * ERING + ERING + r, r, partitions[r])

            with sp.Fori(0, NBODY - 2) as i:
                turn(i, [P] * ERING)
            turn(NBODY - 2, [P] * (ERING - 1) + [GTAIL // GJ])
            turn(NBODY - 1, None)

            for c in range(2):
                sp.wait_ge(stored[c], 16 * NBODY)
            sp.wait_ge(win_done, NWIN + AHEAD)
            sp.wait_ge(e_added, NG + AHEAD)

            def load_weights(k):
                sp.dma_start(unat, U_W[k, :, :]).then_inc(w_in, 16)
                sp.dma_start(ihnat, Wih[k, :, :].rearrange("(g a) b -> a g b", a=P)).then_inc(w_in, 16)
                sp.dma_start(hhnat, Whh[k, :, :].rearrange("(g a) b -> a g b", a=P)).then_inc(w_in, 16)
                sp.dma_start(bnat[:, 0:1], U_b[k, :].rearrange("(a o) -> a o", o=1)).then_inc(w_in, 16)
                sp.dma_start(bnat[:, 1:4], bih[k, :].rearrange("(g a) -> a g", a=P), allow_slow_non_contiguous=True).then_inc(w_in, 16)
                sp.dma_start(bnat[:, 4:7], bhh[k, :].rearrange("(g a) -> a g", a=P), allow_slow_non_contiguous=True).then_inc(w_in, 16)

            def load_half(m, j, J, c):
                wait(sp, prod_done, J - 1)
                sp.dma_start(strm[c].rearrange("p b s d -> p b (s d)"),
                             mat_dram[bass.ds(j * HB, HB), m, :, :].rearrange("b p n -> p b n")
                             ).then_inc(strm_in[c], 16)

            load_weights(0)
            for k in range(ROUNDS + 1):
                m = 0 if k < ROUNDS else 1
                for c in range(2):
                    load_half(m, c, k * NHALF + c, c)
                if 0 < k < ROUNDS:
                    sp.wait_ge(h_ready, k * NHALF + AHEAD)
                    load_weights(k)
                with sp.Fori(1, NSUP) as i:
                    for c in range(2):
                        load_half(m, i * 2 + c, i * 2 + (k * NHALF + c), c)

            for b in range(NTB):
                t0, n = batch(b)
                sp.wait_ge(res_ready, b + 1)
                if (t0 + n) * P <= N:
                    sp.dma_start(out[t0 * P:(t0 + n) * P, :].rearrange("(t p) f -> p t f", p=P),
                                 h_nat[:, t0:t0 + n, :]).then_inc(out_stored, 16)
                else:
                    sp.dma_start(out[t0 * P:N, :], h_nat[0:N - t0 * P, t0, :]).then_inc(out_stored, 16)
            sp.wait_ge(out_stored, 16 * NTB)

        @block.gpsimd
        def _(pool):
            def iota(out_ap, pattern, base=0, channel=0):
                return nc.gpsimd.iota(out_ap, pattern=pattern, base=base, channel_multiplier=channel,
                                      allow_small_or_imprecise_dtypes=True)

            nc.gpsimd.memset(x_nat[:, HI - 1, :], 0.0).then_inc(xpad_ready, 1)
            nc.gpsimd.memset(ident[:, :], 0.0).then_inc(const_ready, 1)
            nc.gpsimd.memset(ebuf[:, :, :, :], 1.0).then_inc(const_ready, 1)
            pool.wait_ge(const_ready, 1)
            nc.gpsimd.memset(ones[:, :], 1.0)
            nc.gpsimd.affine_select(out=ident[:, :], in_=ident[:, :], compare_op=ALU.not_equal, fill=1.0, base=0,
                                    pattern=[[-1, P]], channel_multiplier=1).then_inc(const_ready, 1)
            iota(iotaLo[:, :], [[1, P]])
            iota(iotaKey[:, :], [[1, KEYS]])
            iota(iotaS[:, :], [[1, SW]])
            iota(further[:, :], [[-SW, N // SW + 1]], base=-SW)
            iota(winLo[:, :], [[WPT * WD, WT]], channel=WD)
            iota(winHi[:, :], [[WPT * WD, WT]], base=WD - 1, channel=WD)
            iota(cLess[:, :], [[-1, NCP]], base=int(BIG))
            iota(cPlus[:, :], [[1, NCP]], base=1)
            nc.gpsimd.memset(zrow[:, :], 0.0).then_inc(const_ready, 1)
            iota(winBase[:, :], [[KEYS, NWIN]])
            nc.gpsimd.memset(sumE[:, :], 0.0)
            nc.gpsimd.memset(eaw[:, :], 0.0).then_inc(const_ready, 1)

            pool.wait_ge(dst_stored, 16)
            pool.wait_ge(idx_ready, 1)
            for k in range(2):
                for q in range(WT):
                    nc.gpsimd.indirect_dma_start(
                        out=gath[0:WPT, k, q, :], out_offset=None, in_=dst_dram[:, :],
                        in_offset=bass.IndirectOffsetOnAxis(ap=rowIdx[0:WPT, k, q:q + 1], axis=0)).then_inc(gathered, 16)

            pool.wait_ge(tables_ready, 1)

            def per_row(w, j0, j1, f):
                return recs[:, w, j0:j1, f:f + 1].broadcast_to([P, j1 - j0, P])

            with pool.Fori(0, NBODY) as i:
                for u in range(WPTURN):
                    w, s = i * WPTURN + u, u % 2
                    pool.wait_ge(hot0_ready, w + 1)
                    nc.gpsimd.tensor_tensor(hot[s][1][:, 0:1, :], hot[s][0][:, 0:1, :], per_row(u, 0, 1, 2), ALU.mult)
                    nc.gpsimd.tensor_tensor(hot[s][3], hot[s][0], per_row(u, 0, STEP, 4),
                                            ALU.mult).then_inc(hot3_ready, 1)

        @block.scalar
        def _(act):
            act.sem_inc(win_out, AHEAD)
            act.wait_ge(lam_ready, 2)
            act.wait_ge(rows_in, 15 * 16)
            nc.scalar.activation(rowW, rowDt, ACT.Exp, scale=lamN[:, 0:1]).then_inc(decay_ready, 1)
            act.wait_ge(int_ready, 1)
            nc.scalar.copy(rowRec[:, :, :, 0], rowLoI)
            for q in range(3):
                act.wait_ge(part_ready, q + 1)
                last = nc.scalar.copy(rowRec[:, :, :, 2 + q], wbf[q])
            act.wait_ge(key_ready, 1)
            last.then_inc(recs_ready, 1)
            act.wait_ge(var_ready, 1)
            nc.scalar.activation(rstd[:, :], mv[:, :, 1], ACT.Sqrt).then_inc(std_ready, 1)

            def norm_apply(n):
                act.wait_ge(scale_ready, n)
                for t in range(HI):
                    nc.scalar.activation(h_nat[:, t, :], x_nat[:, t, :], ACT.Relu, bias=mscale[:, t:t + 1],
                                         scale=rstd[:, t:t + 1]).then_inc(norm_ready, 1)

            norm_apply(1)
            for b in range(NTB):
                t0, n = batch(b)
                act.wait_ge(t_done, b + 1)
                nc.scalar.copy(hT[:, t0 * P:(t0 + n) * P], bank[6 + b % 2][:, 0:n * P]).then_inc(t_out, 1)

            def window_out(i, u):
                w, s, c = i * WPTURN + u, u % 2, u // WPB
                if u % WPB == 0:
                    with act.If(i > 0):
                        act.wait_ge(stored[c], i * 16)
                        act.sem_inc(stages, 1)
                act.wait_ge(win_done, w + 1 + AHEAD)
                d = u % WPB * WD
                for m, ps in enumerate((psC, psW)):
                    last = nc.scalar.copy(stage[c][:, m, :, d:d + WD],
                                          ps[s][:, 0:KEYS].rearrange("p (d s) -> p s d", s=HI))
                last.then_inc(win_out, 1)
                if u % WPB == WPB - 1:
                    act.wait_ge(win_out, w + 1 + AHEAD)
                    act.wait_ge(block_ready, i * 2 + (c + 1))
                    act.dma_start(mat_dram[bass.ds(i * 2 + c, 1), :, :, :].rearrange("o m p n -> p (o m) n"),
                                  stage[c].rearrange("p m s d -> p m (s d)")).then_inc(stored[c], 16)

            act.wait_ge(tables_ready, 1)
            with act.Fori(0, NBODY) as i:
                for u in range(WPTURN):
                    w, s = i * WPTURN + u, u % 2
                    act.wait_ge(hot0_ready, w + 1)
                    for j in range(STEP):
                        last = nc.scalar.activation(hot[s][2][:, j, :], hot[s][0][:, j, :], ACT.Copy,
                                                    scale=recs[:, u, j, 3:4])
                    last.then_inc(hot2_ready, 1)
                    if u > 0:
                        window_out(i, u - 1)
                window_out(i, WPTURN - 1)

            for j in range(NHALF):
                act.wait_ge(deg_spread, j + 1)
                nc.scalar.copy(degB[:, j * HALF:(j + 1) * HALF], bank[6 + j % 2][:, 0:HALF]).then_inc(deg_out, 1)

            def product_out(J, c):
                act.wait_ge(prod_done, J + 1)
                nc.scalar.copy(agg0[c][:, :], psP[c][:, 0:HALF]).then_inc(prod_out, 1)

            def message_out(J, c):
                act.wait_ge(msg_done, J + 1)
                nc.scalar.copy(agg[c][:, :], psM[:, 0:HALF]).then_inc(agg_ready, 1)

            def gates(J, c):
                act.wait_ge(gates_done, J + 1)
                nc.scalar.activation(gate[:, 0, :], psR[:, 0:HALF], ACT.Sigmoid, bias=brz[:, 0:1])
                nc.scalar.activation(gate[:, 1, :], psZ[:, 0:HALF], ACT.Sigmoid, bias=brz[:, 1:2]).then_inc(rz_ready, 1)
                act.wait_ge(cand_in, J + 1)
                nc.scalar.activation(gate[:, 2, :], gate[:, 3, :], ACT.Tanh, bias=bnat[:, 3:4]).then_inc(cand_ready, 1)

            for k in range(ROUNDS):
                for b in range(3):
                    act.wait_ge(w_turned, 3 * k + b + 1)
                    nc.scalar.copy(wts[:, 3 * b:3 * b + 3, :],
                                   bank[5 + b][:, 0:3 * F].rearrange("p (g c) -> p g c", g=3)).then_inc(w_ready, 1)
                J = k * NHALF
                product_out(J, 0)
                product_out(J + 1, 1)
                message_out(J, 0)
                with act.Fori(1, NSUP) as i:
                    for c in range(2):
                        product_out(i * 2 + (J + c), c)
                        message_out(i * 2 + (J + c - 1), 1 - c)
                        gates(i * 2 + (J + c - 2), c)
                J += NHALF
                message_out(J - 1, 1)
                gates(J - 2, 0)
                gates(J - 1, 1)
                if k < ROUNDS - 1:
                    for b in range(NTB):
                        t0, n = batch(b)
                        act.wait_ge(t_done, NTB * (k + 1) + b + 1)
                        nc.scalar.copy(h_nat[:, t0:t0 + n, :],
                                       bank[6 + b % 2][:, 0:n * P].rearrange("p (t f) -> p t f", f=F)).then_inc(t_out, 1)
            act.wait_ge(var_ready, 2)
            nc.scalar.activation(rstd[:, :], mv[:, :, 1], ACT.Sqrt).then_inc(std_ready, 1)
            norm_apply(2)
            with act.Fori(0, NSUP) as i:
                for c in range(2):
                    act.wait_ge(prod_done, i * 2 + (ROUNDS * NHALF + c + 1))
                    nc.scalar.copy(hT[:, bass.ds(i * (2 * HALF) + c * HALF, HALF)], psP[c][:, 0:HALF]).then_inc(prod_out, 1)

        @block.vector
        def _(dve):
            steps = [0]

            def link(ins):
                steps[0] += 1
                ins.then_inc(step_done, 1)
                dve.wait_ge(step_done, steps[0])

            dve.sem_inc(e_added, AHEAD)
            dve.sem_inc(ex_added, AHEAD)
            dve.sem_inc(h_ready, AHEAD)
            nc.vector.memset(rowDst, NODST)
            nc.vector.memset(rowSrc, 0)
            nc.vector.memset(rowG, NODST).then_inc(pad_ready, 1)
            nc.vector.memset(rowDt, 0.0)
            nc.vector.memset(rowNorm, 0.0).then_inc(pad_ready, 1)
            dve.wait_ge(small_in, 32)
            nc.vector.tensor_scalar(lamN[:, :], lamB[:, :], 0.0, 1e-4, ALU.max, ALU.add).then_inc(lam_ready, 1)
            dve.wait_ge(lam_ready, 1)
            nc.vector.tensor_scalar(lamN[:, :], lamN[:, :], -1.0, None, ALU.mult).then_inc(lam_ready, 1)

            dve.wait_ge(rows_in, 15 * 16)
            nc.vector.tensor_reduce(chMM[:, 0, :], rowDst, AX.X, ALU.min)
            nc.vector.tensor_reduce(chMM[:, 1, :], rowDst, AX.X, ALU.max)
            nc.vector.tensor_single_scalar(rowLoI, rowSrc, P - 1, ALU.bitwise_and).then_inc(int_ready, 1)
            dve.wait_ge(int_ready, 1)
            dve.wait_ge(const_ready, 3)

            def diagonal(n, value, size):
                wait(dve, diag_spread, n - 1)
                nc.vector.tensor_scalar(diag[0:size, n % 2, 0:size], ident[0:size, 0:size], value, None,
                                        ALU.mult).then_inc(diag_ready, 1)

            for k in range(2):
                for t in range(CT):
                    diagonal(k * CT + t, chMM[:, k, t:t + 1], P)
            dve.wait_ge(decay_ready, 1)
            nc.vector.tensor_single_scalar(rowHi, rowSrc, 7, ALU.arith_shift_right)
            link(nc.vector.tensor_tensor(rowW, rowW, rowNorm, ALU.mult))
            for q in range(3):
                nc.vector.tensor_copy(wbf[q], rowW).then_inc(part_ready, 1)
                if q == 0:
                    nc.vector.scalar_tensor_tensor(rowRec[:, :, :, 1], rowDst, float(HI), rowHi, ALU.mult,
                                                   ALU.add).then_inc(key_ready, 1)
                if q < 2:
                    dve.wait_ge(part_ready, q + 1)
                    link(nc.vector.tensor_tensor(rowW, rowW, wbf[q], ALU.subtract))
            for k, dest in enumerate((chMinB, chMaxB)):
                dve.wait_ge(diag_spread, CT * (k + 1))
                nc.vector.tensor_copy(dest[:, 0:512], bank[2 * k][:, :])
                nc.vector.tensor_copy(dest[:, 512:NCP], bank[2 * k + 1][:, 0:NCP - 512]).then_inc(spread_out, 1)
            dve.wait_ge(spread_out, 2)
            dve.wait_ge(const_ready, 4)
            W, C = slice(0, WPT), slice(0, NCH)
            for q in range(WT):
                link(nc.vector.tensor_scalar(m0[W, C], chMinB[W, C], winHi[W, q:q + 1], None, ALU.is_le))
                link(nc.vector.scalar_tensor_tensor(m1[W, C], chMaxB[W, C], winLo[W, q:q + 1], m0[W, C],
                                                    ALU.is_ge, ALU.mult))
                for k, factor in enumerate((cLess, cPlus)):
                    ins = nc.vector.tensor_tensor_reduce(out=m0[W, C], in0=m1[W, C], in1=factor[W, C], scale=1.0,
                                                         scalar=0.0, op0=ALU.mult, op1=ALU.max,
                                                         accum_out=loHi[W, k, q:q + 1])
                    link(ins)
            link(nc.vector.tensor_scalar(loHi[W, 0, :], loHi[W, 0, :], -1.0, BIG, ALU.mult, ALU.add))
            link(nc.vector.tensor_scalar(loHi[W, 0, :], loHi[W, 0, :], float(NCH), None, ALU.min))
            link(nc.vector.tensor_scalar(loHi[W, 1, :], loHi[W, 1, :], -1.0, 0.0, ALU.add, ALU.max))
            nc.vector.tensor_copy(rowIdx[W, :, :], loHi[W, :, :]).then_inc(idx_ready, 1)

            nc.vector.tensor_reduce(gMM[0:GPT, 0, :], rowG[0:GPT], AX.X, ALU.min)
            nc.vector.tensor_reduce(gMM[0:GPT, 1, :], rowG[0:GPT], AX.X, ALU.max)
            link(nc.vector.tensor_copy(rowGf[0:GPT], rowG[0:GPT]))
            link(nc.vector.tensor_scalar(gMM[0:GPT], gMM[0:GPT], float(N - 1), None, ALU.min))
            for t in range(GT):
                diagonal(2 * CT + t, gMM[0:GPT, 0, t:t + 1], GPT)

            def norm_stats(n):
                for t in range(HI):
                    last = nc.vector.bn_stats(stats[:, t, :], x_nat[:, t, :])
                link(last)
                for t in range(HI):
                    last = nc.vector.bn_aggr(mv[:, t, :], stats[:, t, :])
                link(last)
                nc.vector.tensor_scalar(mv[:, :, 1], mv[:, :, 1], EPS, None, ALU.add).then_inc(var_ready, 1)
                dve.wait_ge(std_ready, n)
                link(nc.vector.reciprocal(rstd[:, :], rstd[:, :]))
                nc.vector.scalar_tensor_tensor(mscale[:, :], mv[:, :, 0], -1.0, rstd[:, :], ALU.mult,
                                               ALU.mult).then_inc(scale_ready, 1)

            dve.wait_ge(x_in, 32)
            norm_stats(1)

            dve.wait_ge(grp_turned, 1)
            link(nc.vector.tensor_copy(dstG[:, :, 0], bank[4][:, 0:NG]))
            for j in range(GJ - 1, -1, -1):
                nc.vector.tensor_tensor(dstG[:, :, j], bank[5 + j // 2][:, (j % 2) * NG:(j % 2 + 1) * NG],
                                        dstG[:, :, 0], ALU.subtract)

            dve.wait_ge(gathered, 2 * WT * 16)
            lows = winLo[W, :].rearrange("p (q o) -> p q o", o=1).broadcast_to([WPT, WT, P])
            for k in range(2):
                last = nc.vector.tensor_tensor(rel[W, k, :, :], gath[W, k, :, :], lows, ALU.subtract)
            link(last)
            inside = gath.bitcast(f32)
            link(nc.vector.tensor_scalar(inside[W], rel[W], 0.0, None, ALU.is_ge))
            link(nc.vector.scalar_tensor_tensor(inside[W], rel[W], float(WD - 1), inside[W], ALU.is_le, ALU.mult))
            for k, factor in enumerate((cLess, cPlus)):
                f = factor[W, 0:P].rearrange("p (o e) -> p o e", o=1).broadcast_to([WPT, WT, P])
                last = nc.vector.tensor_tensor(rel[W, k, :, :], inside[W, k, :, :], f, ALU.mult)
            link(last)
            link(nc.vector.tensor_reduce(posLH[W, :, :], rel[W], AX.X, ALU.max))
            link(nc.vector.tensor_scalar(posLH[W, 0, :], posLH[W, 0, :], -1.0, BIG, ALU.mult, ALU.add))
            link(nc.vector.tensor_scalar(posLH[W, 0, :], posLH[W, 0, :], float(P), None, ALU.min))
            link(nc.vector.scalar_tensor_tensor(posLH[W, :, :], loHi[W, :, :], float(P), posLH[W, :, :],
                                                ALU.mult, ALU.add))
            nc.vector.tensor_copy(colTab[W, 0, :], posLH[W, 0, :])
            link(nc.vector.tensor_tensor(posLH[W, 1, :], posLH[W, 1, :], posLH[W, 0, :], ALU.subtract))
            link(nc.vector.tensor_scalar(posLH[W, 1, :], posLH[W, 1, :], float(P - 1 - TAKE), 0.0, ALU.add, ALU.max))
            link(nc.vector.tensor_copy(colInt[W, :], posLH[W, 1, :]))
            link(nc.vector.tensor_single_scalar(colInt[W, :], colInt[W, :], 7, ALU.arith_shift_right))
            nc.vector.tensor_copy(colTab[W, 1, :], colInt[W, :]).then_inc(lohi_ready, 1)

            dve.wait_ge(lohi_turned, 1)
            R = [rowTab[:, n, :] for n in range(4)]
            nc.vector.tensor_copy(startTab[:, :], bank[0][0:1, 0:NWIN])
            nc.vector.tensor_copy(R[1], bank[1][0:1, 0:NWIN])
            nc.vector.tensor_copy(R[0][:, 0:NG], bank[2][0:1, 0:NG])
            link(nc.vector.tensor_copy(R[3][:, 0:NG], bank[2][0:1, NG:2 * NG]))
            nc.vector.tensor_copy(furtherTab[:, :], R[1])
            quadSum, turnSum = R[3][:, NG:NG + NQ], R[3][:, NG + NQ:NG + NQ + NBODY]
            nc.vector.tensor_reduce(quadSum, R[1].rearrange("p (q v) -> p q v", v=QUAD), AX.X, ALU.add)
            link(nc.vector.tensor_tensor_scan(R[2], R[1], zrow[:, :], 0.0, ALU.add, ALU.add))
            link(nc.vector.tensor_tensor(beforeTab[:, :], R[2], R[1], ALU.subtract))
            G = [rowTab[:, n, 0:NG] for n in range(4)]
            nc.vector.memset(grpFirst[:, :, ERING:8], 0)
            nc.vector.tensor_copy(grpFirst[:, :, 0:ERING], G[0].rearrange("p (b r) -> p b r", r=ERING))
            link(nc.vector.tensor_tensor(grpFurther[:, :], G[3], G[0], ALU.subtract))
            link(nc.vector.tensor_single_scalar(grpFurther[:, :], grpFurther[:, :], 5, ALU.arith_shift_right))
            link(nc.vector.tensor_copy(G[1], grpFurther[:, :]))
            nc.vector.tensor_copy(quadTab[:, :], quadSum)
            nc.vector.tensor_reduce(turnSum, G[1].rearrange("p (b r) -> p b r", r=ERING), AX.X, ALU.add)
            link(nc.vector.tensor_tensor_scan(G[2], G[1], zrow[:, 0:NG], 0.0, ALU.add, ALU.add))
            nc.vector.tensor_copy(turnTab[:, :], turnSum)
            nc.vector.tensor_tensor(grpBefore[:, :], G[2], G[1], ALU.subtract).then_inc(tables_ready, 1)

            def rows_of(ap):
                return ap.rearrange("p (j o) -> p j o", o=1).broadcast_to([P, GJ, SW])

            along = iotaS[:, :].rearrange("p (o c) -> p o c", o=1).broadcast_to([P, GJ, SW])

            def quad_keys(i, k):
                dve.wait_ge(rec_in[k], i * (QUAD * 16) + QUAD * 16)
                sl = slice(k * QUAD, (k + 1) * QUAD)
                base = winBase[:, bass.ds(i * WPTURN + k * QUAD, QUAD)]
                nc.vector.tensor_tensor(keyrel[:, sl, :], recs[:, sl, :, 1],
                                        base.rearrange("p (w o) -> p w o", o=1).broadcast_to([P, QUAD, STEP]),
                                        ALU.subtract).then_inc(keyrel_ready, 1)
                dve.wait_ge(keyrel_ready, i * QPB + (k + 1))

            def window_hot(i, u):
                w, s = i * WPTURN + u, u % 2
                dve.wait_ge(win_done, w - 1 + AHEAD)
                for j in range(STEP):
                    last = nc.vector.tensor_scalar(hot[s][0][:, j, :], iotaLo[:, :], recs[:, u, j, 0:1], None,
                                                   ALU.is_equal)
                last.then_inc(hot0_ready, 1)
                nc.vector.tensor_scalar(hot[s][1][:, 1, :], iotaLo[:, :], recs[:, u, 1, 0:1], recs[:, u, 1, 2:3],
                                        ALU.is_equal, ALU.mult)
                for j in range(STEP):
                    last = nc.vector.tensor_scalar(key[s][:, j, 0:KEYS], iotaKey[:, :], keyrel[:, u, j:j + 1], None,
                                                   ALU.is_equal)
                last.then_inc(hot1_ready, 1)

            def further_edges(i, k):
                any_further = dve.value_load(quadTab[0:1, bass.ds(i * QPB + k, 1)], min_val=0, max_val=NCH * QUAD)
                with dve.If(any_further > 0):
                    for v in range(QUAD):
                        u = k * QUAD + v
                        w, c, d = i * WPTURN + u, u // WPB, u % WPB * WD
                        nx = dve.value_load(furtherTab[0:1, bass.ds(w, 1)], min_val=0, max_val=NCH)
                        with dve.If(nx > 0):
                            xb = dve.value_load(beforeTab[0:1, bass.ds(w, 1)], min_val=0, max_val=NCH * NWIN)
                            with dve.Fori(0, nx) as n:
                                dve.wait_ge(xrec_in, (xb + n) * 16 + 16)
                                nc.vector.tensor_tensor(xkeyrel, xrec[:, 1:2], winBase[:, bass.ds(w, 1)],
                                                        ALU.subtract).then_inc(xkeyrel_ready, 1)
                                dve.wait_ge(xkeyrel_ready, xb + n + 1)
                                nc.vector.tensor_scalar(xhot[0], iotaLo[:, :], xrec[:, 0:1], None, ALU.is_equal)
                                for q in range(3):
                                    nc.vector.tensor_scalar(xhot[q + 1], iotaLo[:, :], xrec[:, 0:1],
                                                            xrec[:, 2 + q:3 + q], ALU.is_equal, ALU.mult)
                                nc.vector.tensor_scalar(xkey[:, 0:KEYS], iotaKey[:, :], xkeyrel, None,
                                                        ALU.is_equal).then_inc(xhot_ready, 1)
                                dve.wait_ge(xhot_used, xb + n + 1 + AHEAD)
                                dve.wait_ge(win_out, w + 1 + AHEAD)
                                for m, ps in enumerate((psXC, psXW)):
                                    part = stage[c][:, m, :, d:d + WD]
                                    last = nc.vector.tensor_tensor(
                                        part, part, ps[:, 0:KEYS].rearrange("p (d s) -> p s d", s=HI), ALU.add)
                                last.then_inc(x_added, 1)
                                dve.wait_ge(x_added, xb + n + 1)
                if k % 2 == 1:
                    dve.sem_inc(block_ready, 1)

            def group_rel(g):
                return dstG[:, bass.ds(g, 1), :].rearrange("p o j -> p (o j)")

            def further_groups(i):
                any_further = dve.value_load(turnTab[0:1, bass.ds(i, 1)], min_val=0, max_val=ERING * (N // SW))
                with dve.If(any_further > 0):
                    for r in range(ERING):
                        g = i * ERING + r
                        nx = dve.value_load(grpFurther[0:1, bass.ds(g, 1)], min_val=0, max_val=N // SW)
                        with dve.If(nx > 0):
                            xb = dve.value_load(grpBefore[0:1, bass.ds(g, 1)], min_val=0, max_val=NG * (N // SW))
                            d0 = dve.value_load(grpFirst[0:1, bass.ds(i, 1), r:r + 1], min_val=0, max_val=N - 1)
                            with dve.Fori(0, nx) as n:
                                nc.vector.tensor_scalar(exrel, group_rel(g), further[:, bass.ds(n, 1)], None,
                                                        ALU.add).then_inc(exrel_ready, 1)
                                dve.wait_ge(exrel_ready, xb + n + 1)
                                nc.vector.tensor_tensor(exhot, along, rows_of(exrel),
                                                        ALU.is_equal).then_inc(exhot_ready, 1)
                                dve.wait_ge(ex_done, xb + n + 1)
                                dve.wait_ge(e_added, i * ERING + AHEAD)
                                dve.wait_ge(ex_added, xb + n + AHEAD)
                                cols = bass.ds(nc.s_assert_within(d0 + n * SW + SW, 0, N - 1), SW)
                                nc.vector.tensor_tensor(sumE[:, cols], sumE[:, cols], psXC[0:EA, 0:SW],
                                                        ALU.add).then_inc(ex_added, 1)
                                dve.wait_ge(ex_added, xb + n + 1 + AHEAD)

            def group_hot(i, r):
                nc.vector.tensor_tensor(ehot[r], along, rows_of(group_rel(i * ERING + r)),
                                        ALU.is_equal).then_inc(ehot_ready, 1)

            def group_add(i, r, d0):
                g = i * ERING + r
                dve.wait_ge(e_used, g + 1)
                dve.wait_ge(e_added, g + AHEAD)
                nc.vector.tensor_tensor(sumE[:, bass.ds(d0, SW)], sumE[:, bass.ds(d0, SW)],
                                        psE[r % 2][0:EA, r // 2 * SW:(r // 2 + 1) * SW], ALU.add).then_inc(e_added, 1)

            regs, held = entry_regs(dve, "dve"), {}
            dve.wait_ge(tables_ready, 1)
            dve.wait_ge(const_ready, 5)
            with dve.Fori(0, NBODY) as i:
                further_groups(i)
                for u in range(WPTURN):
                    if u % QUAD == 0:
                        quad_keys(i, u // QUAD)
                    if u % 8 == 1:
                        at = u // 8 * 4
                        first = read4(dve, regs, grpFirst[0:1, bass.ds(i, 1), at:at + 4], N - 1)
                        held.update({at + n: first[n] for n in range(4)})
                    window_hot(i, u)
                    if u % 2 == 1 and u // 2 < ERING:
                        group_hot(i, u // 2)
                    if u % 2 == 0 and 2 <= u <= 2 * ERING:
                        group_add(i, u // 2 - 1, held[u // 2 - 1])
                    if u % QUAD == 0 and u > 0:
                        further_edges(i, u // QUAD - 1)
                further_edges(i, QPB - 1)

            def weights(k):
                dve.wait_ge(w_in, 16 * 6 * (k + 1))
                nc.vector.tensor_copy(eaw[:, 0:FE], unat[:, 2 * F:2 * F + FE])
                nc.vector.tensor_tensor(brz[:, 0:2], bnat[:, 1:3], bnat[:, 4:6], ALU.add)
                link(nc.vector.scalar_tensor_tensor(cbv[:, 0:1], condB[:, 0:1], unat[:, 2 * F + FE:2 * F + FE + 1],
                                                    bnat[:, 0:1], ALU.mult, ALU.add))
                nc.vector.scalar_tensor_tensor(eaw[:, FE:FE + 1], condB[:, 1:2], unat[:, 2 * F + FE + 1:2 * F + FE + 2],
                                               cbv[:, 0:1], ALU.mult, ALU.add).then_inc(w_prep, 1)

            def times_degree(j, J, c):
                wait(dve, msg_done, J - 1)
                cols = bass.ds(j * HALF, HALF)
                nc.vector.tensor_tensor(hdeg[c][:, :], hT[:, cols], degB[:, cols], ALU.mult).then_inc(hdeg_ready, 1)

            def update(j, J):
                cols = bass.ds(j * HALF, HALF)
                dve.wait_ge(rz_ready, J + 1)
                nc.vector.scalar_tensor_tensor(gate[:, 3, :], psH[:, 0:HALF], bnat[:, 6:7], gate[:, 0, :],
                                               ALU.add, ALU.mult).then_inc(gru_step, 1)
                dve.wait_ge(gru_step, J * 3 + 1)
                nc.vector.tensor_tensor(gate[:, 3, :], gate[:, 3, :], psI[:, 0:HALF], ALU.add).then_inc(cand_in, 1)
                dve.wait_ge(cand_ready, J + 1)
                nc.vector.tensor_tensor(gate[:, 3, :], hT[:, cols], gate[:, 2, :], ALU.subtract).then_inc(gru_step, 1)
                dve.wait_ge(gru_step, J * 3 + 2)
                nc.vector.tensor_tensor(gate[:, 3, :], gate[:, 3, :], gate[:, 1, :], ALU.mult).then_inc(gru_step, 1)
                dve.wait_ge(gru_step, J * 3 + 3)
                nc.vector.tensor_tensor(hT[:, cols], gate[:, 2, :], gate[:, 3, :], ALU.add).then_inc(h_ready, 1)

            dve.wait_ge(deg_out, NHALF)
            for k in range(ROUNDS):
                weights(k)
                J = k * NHALF
                dve.wait_ge(h_ready, J + AHEAD)
                times_degree(0, J, 0)
                times_degree(1, J + 1, 1)
                with dve.Fori(1, NSUP) as i:
                    for c in range(2):
                        times_degree(i * 2 + c, i * 2 + (J + c), c)
                        update(i * 2 + (c - 2), i * 2 + (J + c - 2))
                J += NHALF
                update(NHALF - 2, J - 2)
                update(NHALF - 1, J - 1)

            for b in range(NTB):
                t0, n = batch(b)
                dve.wait_ge(t_done, NTB * (ROUNDS + 0) + b + 1)
                last = nc.vector.tensor_tensor(x_nat[:, t0:t0 + n, :], x_nat[:, t0:t0 + n, :],
                                               bank[6 + b % 2][:, 0:n * P].rearrange("p (t f) -> p t f", f=F),
                                               ALU.add).then_inc(t_out, 1)
            dve.wait_ge(t_out, NTB * (ROUNDS + 1))
            norm_stats(2)
            for b in range(NTB):
                t0, n = batch(b)
                dve.wait_ge(t_done, NTB * (ROUNDS + 1) + b + 1)
                nc.vector.tensor_tensor(h_nat[:, t0:t0 + n, :], x_nat[:, t0:t0 + n, :],
                                        bank[6 + b % 2][:, 0:n * P].rearrange("p (t f) -> p t f", f=F),
                                        ALU.add).then_inc(res_ready, 1)

        @block.tensor
        def _(pe):
            pe.sem_inc(win_done, AHEAD)
            pe.sem_inc(xhot_used, AHEAD)
            pe.wait_ge(const_ready, 3)
            for k in range(2):
                for t in range(CT):
                    n = k * CT + t
                    pe.wait_ge(diag_ready, n + 1)
                    nc.tensor.matmul(bank[2 * k + t // 4][:, t % 4 * P:(t % 4 + 1) * P], ones[:, :],
                                     diag[:, n % 2, :], start=True, stop=True).then_inc(diag_spread, 1)
            for t in range(GT):
                pe.wait_ge(diag_ready, 2 * CT + t + 1)
                nc.tensor.matmul(bank[4][:, t * GPT:(t + 1) * GPT], ones[0:GPT, :],
                                 diag[0:GPT, (2 * CT + t) % 2, 0:GPT], start=True, stop=True).then_inc(diag_spread, 1)
            for j in range(GJ):
                for t in range(GT):
                    last = nc.tensor.transpose(bank[5 + j // 2][:, (j % 2) * NG + t * GPT:(j % 2) * NG + (t + 1) * GPT],
                                               rowGf[0:GPT, t, bass.ds(j, P, GJ)], ident[0:GPT, 0:GPT])
            last.then_inc(grp_turned, 1)
            pe.wait_ge(lohi_ready, 1)
            for k in range(2):
                for q in range(WT):
                    nc.tensor.matmul(bank[k][0:1, q * WPT:(q + 1) * WPT], colTab[0:WPT, k, q:q + 1],
                                     ident[0:WPT, 0:WPT], start=True, stop=True)
                for t in range(GT):
                    last = nc.tensor.matmul(bank[2][0:1, k * NG + t * GPT:k * NG + (t + 1) * GPT],
                                            gMM[0:GPT, k, t:t + 1], ident[0:GPT, 0:GPT], start=True, stop=True)
            last.then_inc(lohi_turned, 1)

            def turn_tiles(source, n0):
                for b in range(NTB):
                    t0, n = batch(b)
                    if b >= 2:
                        pe.wait_ge(res_ready if n0 > NTB * ROUNDS else t_out,
                                   b - 1 if n0 > NTB * ROUNDS else n0 + b - 1)
                    for t in range(n):
                        last = nc.tensor.transpose(bank[6 + b % 2][:, t * P:(t + 1) * P], source(t0 + t), ident[:, :])
                    last.then_inc(t_done, 1)

            pe.wait_ge(norm_ready, HI)
            turn_tiles(lambda t: h_nat[:, t, :], 0)
            pe.wait_ge(tables_ready, 1)
            pe.wait_ge(t_out, NTB)

            def further_edges(i, k):
                any_further = pe.value_load(quadTab[0:1, bass.ds(i * QPB + k, 1)], min_val=0, max_val=NCH * QUAD)
                with pe.If(any_further > 0):
                    for v in range(QUAD):
                        w = i * WPTURN + (k * QUAD + v)
                        nx = pe.value_load(furtherTab[0:1, bass.ds(w, 1)], min_val=0, max_val=NCH)
                        with pe.If(nx > 0):
                            xb = pe.value_load(beforeTab[0:1, bass.ds(w, 1)], min_val=0, max_val=NCH * NWIN)
                            with pe.Fori(0, nx) as n:
                                pe.wait_ge(xhot_ready, xb + n + 1)
                                nc.tensor.matmul(psXC[:, 0:KEYS], xhot[0], xkey[:, 0:KEYS], start=True, stop=True)
                                for q in range(3):
                                    last = nc.tensor.matmul(psXW[:, 0:KEYS], xhot[q + 1], xkey[:, 0:KEYS],
                                                            start=q == 0, stop=q == 2)
                                last.then_inc(xhot_used, 1)

            def window(i, u):
                w, s = i * WPTURN + u, u % 2
                pe.wait_ge(hot1_ready, w + 1)
                pe.wait_ge(win_out, w - 1 + AHEAD)
                for j in range(STEP):
                    nc.tensor.matmul(psC[s][:, 0:KEYS], hot[s][0][:, j, :], key[s][:, j, 0:KEYS],
                                     start=j == 0, stop=j == STEP - 1)
                pe.wait_ge(hot2_ready, w + 1)
                pe.wait_ge(hot3_ready, w + 1)
                for j in range(STEP):
                    for q in range(3):
                        last = nc.tensor.matmul(psW[s][:, 0:KEYS], hot[s][q + 1][:, j, :], key[s][:, j, 0:KEYS],
                                                start=j == 0 and q == 0, stop=j == STEP - 1 and q == 2)
                last.then_inc(win_done, 1)

            def further_groups(i):
                any_further = pe.value_load(turnTab[0:1, bass.ds(i, 1)], min_val=0, max_val=ERING * (N // SW))
                with pe.If(any_further > 0):
                    for r in range(ERING):
                        g = i * ERING + r
                        nx = pe.value_load(grpFurther[0:1, bass.ds(g, 1)], min_val=0, max_val=N // SW)
                        with pe.If(nx > 0):
                            xb = pe.value_load(grpBefore[0:1, bass.ds(g, 1)], min_val=0, max_val=NG * (N // SW))
                            with pe.Fori(0, nx) as n:
                                pe.wait_ge(e_in[r], i * 16 + 16)
                                pe.wait_ge(exhot_ready, xb + n + 1)
                                for j in range(GJ):
                                    last = nc.tensor.matmul(psXC[0:EA, 0:SW], ebuf[:, r, j, :], exhot[:, j, :],
                                                            start=j == 0, stop=j == GJ - 1)
                                last.then_inc(ex_done, 1)

            def group(i, r):
                g = i * ERING + r
                pe.wait_ge(e_in[r], i * 16 + 16)
                pe.wait_ge(ehot_ready, g + 1)
                pe.wait_ge(e_added, g - 1 + AHEAD)
                for j in range(GJ):
                    last = nc.tensor.matmul(psE[r % 2][0:EA, r // 2 * SW:(r // 2 + 1) * SW], ebuf[:, r, j, :],
                                            ehot[r][:, j, :], start=j == 0, stop=j == GJ - 1)
                last.then_inc(e_used, 1)

            with pe.Fori(0, NBODY) as i:
                further_groups(i)
                for u in range(WPTURN):
                    window(i, u)
                    if u % 2 == 1 and u // 2 < ERING:
                        group(i, u // 2)
                    if u % QUAD == 0 and u > 0:
                        further_edges(i, u // QUAD - 1)
                further_edges(i, QPB - 1)

            pe.wait_ge(e_added, NG + AHEAD)
            for j in range(NHALF):
                if j >= 2:
                    pe.wait_ge(deg_out, j - 1)
                nc.tensor.matmul(bank[6 + j % 2][:, 0:HALF], ones[FE:FE + 1, :],
                                 sumE[FE:FE + 1, j * HALF:(j + 1) * HALF], start=True, stop=True).then_inc(deg_spread, 1)
            pe.wait_ge(deg_out, NHALF)
            pe.wait_ge(win_out, NWIN + AHEAD)

            def product(J, c):
                pe.wait_ge(strm_in[c], 8 * (J - c) + 16)
                wait(pe, prod_out, J - 1)
                for s in range(HI):
                    last = nc.tensor.matmul(psP[c][:, 0:HALF], h_nat[:, s, :], strm[c][:, :, s, :],
                                            start=s == 0, stop=s == HI - 1)
                last.then_inc(prod_done, 1)

            def message(j, J, c):
                pe.wait_ge(prod_out, J + 1)
                pe.wait_ge(hdeg_ready, J + 1)
                wait(pe, agg_ready, J)
                nc.tensor.matmul(psM[:, 0:HALF], wts[:, 1, :], agg0[c][:, :], start=True, stop=False)
                nc.tensor.matmul(psM[:, 0:HALF], wts[:, 0, :], hdeg[c][:, :], start=False, stop=False)
                nc.tensor.matmul(psM[:, 0:HALF], wts[0:EA, 2, :], sumE[0:EA, bass.ds(j * HALF, HALF)],
                                 start=False, stop=True).then_inc(msg_done, 1)

            def gru(j, J, c):
                pe.wait_ge(agg_ready, J + 1)
                pe.wait_ge(h_ready, J + AHEAD)
                cols = bass.ds(j * HALF, HALF)
                for g, ps in ((0, psR), (1, psZ)):
                    nc.tensor.matmul(ps[:, 0:HALF], wts[:, 3 + g, :], agg[c][:, :], start=True, stop=False)
                    nc.tensor.matmul(ps[:, 0:HALF], wts[:, 6 + g, :], hT[:, cols], start=False, stop=True)
                nc.tensor.matmul(psI[:, 0:HALF], wts[:, 5, :], agg[c][:, :], start=True, stop=True)
                nc.tensor.matmul(psH[:, 0:HALF], wts[:, 8, :], hT[:, cols], start=True, stop=True).then_inc(gates_done, 1)

            for k in range(ROUNDS):
                pe.wait_ge(w_prep, k + 1)
                wait(pe, t_out, NTB * (k + 1))
                pe.wait_ge(h_ready, k * NHALF + AHEAD)
                raw = [unat[:, 0:F], unat[:, F:2 * F], eaw[:, :]] + [ihnat[:, g, :] for g in range(3)] + \
                      [hhnat[:, g, :] for g in range(3)]
                for n, m in enumerate(raw):
                    last = nc.tensor.transpose(bank[5 + n // 3][:, n % 3 * F:(n % 3 + 1) * F], m, ident[:, :])
                    if n % 3 == 2:
                        last.then_inc(w_turned, 1)
                J = k * NHALF
                product(J, 0)
                product(J + 1, 1)
                pe.wait_ge(w_ready, 3 * (k + 1))
                message(0, J, 0)
                with pe.Fori(1, NSUP) as i:
                    for c in range(2):
                        product(i * 2 + (J + c), c)
                        message(i * 2 + (c - 1), i * 2 + (J + c - 1), 1 - c)
                        gru(i * 2 + (c - 2), i * 2 + (J + c - 2), c)
                J += NHALF
                message(NHALF - 1, J - 1, 1)
                gru(NHALF - 2, J - 2, 0)
                gru(NHALF - 1, J - 1, 1)
                pe.wait_ge(h_ready, J + AHEAD)
                turn_tiles(lambda t: hT[:, t * P:(t + 1) * P], NTB * (k + 1))

            pe.wait_ge(norm_ready, 2 * HI)
            J = ROUNDS * NHALF
            with pe.Fori(0, NSUP) as i:
                for c in range(2):
                    product(i * 2 + (J + c), c)
            pe.wait_ge(prod_out, J + NHALF)
            turn_tiles(lambda t: hT[:, t * P:(t + 1) * P], NTB * (ROUNDS + 1))

    return nc


_ORDER = ["x", "src", "dst", "edge_attr_64", "edge_weight", "edge_weight_n2", "L0_gnn_cond", "L0_gnn_U_W", "L0_gnn_U_b",
          "L0_gnn_Wih", "L0_gnn_Whh", "L0_gnn_bih", "L0_gnn_bhh", "L1_gnn_decay_lam"]


def kernel(**inputs):
    import numpy as np
    import concourse.bacc as bacc
    from concourse.bass_utils import run_bass_kernel_spmd

    nc = bacc.Bacc("TRN2", target_bir_lowering=False, num_devices=1)
    arrays, args = {}, []
    for name in _ORDER:
        a = np.ascontiguousarray(inputs[name])
        arrays[f"in_{name}"] = a
        args.append(nc.dram_tensor(f"in_{name}", a.shape, mybir.dt.from_np(a.dtype), kind="ExternalInput").ap())
    out = nc.dram_tensor("out", (N, F), mybir.dt.float32, kind="ExternalOutput").ap()
    build(nc, *args, out)
    r = run_bass_kernel_spmd(nc, [arrays], core_ids=[0])
    return r.results[0]["out"]
```

```python
import concourse.bass as bass
from concourse import mybir
from contextlib import ExitStack

N, E, F, FE = 3125, 100000, 128, 64
ROUNDS = 3
P = 128
HI = -(-N // P)
NP = HI * P
WD = 7
KEYS = WD * HI
WPB = 8
BD = WPB * WD
BCOLS = HI * BD
NBLK = -(-N // BD)
ND = NBLK * BD
NWIN = NBLK * WPB
QUAD = 4
STEP = 2
TAKE = STEP * P
WT = 4
WPT = NWIN // WT
NCH = -(-E // P)
CT = -(-NCH // P)
NCP = CT * P
FULLCH = E // P
REC = 5
NODST = 4095
BIG = 1024.0
NBODY = NBLK // 2
WPTURN = 2 * WPB
QPB = WPTURN // QUAD
GE = 512
GJ = GE // P
SETS = 4
ERING = 7
GROUP_AT = (0, 1, 2, 5, 8, 11, 13)
FURTHER_AT = 2
NG = NBODY * ERING
GT = 2
GPT = NG // GT
FULLG = E // GE
GTAIL = E - FULLG * GE
ACT_TOO = (0, 2, 4, 8, 12)
EARLY = sum(u <= FURTHER_AT for u in GROUP_AT)
FIRST = 2 * BD
FIRST_FROM = FURTHER_AT + 1
SW = 32
EA = FE + 1
HB = 7
HALF = HB * BD
NHALF = NBLK // HB
NSUP = NHALF // 2
EPS = 1e-5
assert NG == FULLG + 1 and TAKE >= KEYS


def build(nc, x, src, dst, edge_attr, dt_in, norm_in, cond, U_W, U_b, Wih, Whh, bih, bhh, lam, out):
    f32, bf16, i32 = mybir.dt.float32, mybir.dt.bfloat16, mybir.dt.int32
    f16 = mybir.dt.float16
    ALU, ACT, AX = mybir.AluOpType, mybir.ActivationFunctionType, mybir.AxisListType

    ctx = ExitStack()
    with ctx:
        def sb(name, shape, dt=f32):
            return ctx.enter_context(nc.sbuf_tensor(name, shape, dt))

        def pb(name, shape):
            return ctx.enter_context(nc.psum_tensor(name, shape, f32))

        def sem(name):
            return ctx.enter_context(nc.semaphore(name))

        mat_dram = nc.dram_tensor("mat_dram", [NBLK, 2, P, BCOLS], f32, kind="Internal").ap()
        rec_dram = nc.dram_tensor("rec_dram", [NCP * P, REC], f32, kind="Internal").ap()
        dst_dram = nc.dram_tensor("dst_dram", [NCP, P], i32, kind="Internal").ap()

        ident = sb("ident", [P, P])
        ones = sb("ones", [P, P])
        x_nat = sb("x_nat", [P, HI, F])
        h_nat = sb("h_nat", [P, HI, F])
        hT = sb("hT", [P, NP])
        degB = sb("degB", [P, ND])
        sumE = sb("sumE", [EA, ND + SW])
        stats = sb("stats", [P, HI, 6])
        mv = sb("mv", [P, HI, 2])
        rstd = sb("rstd", [P, HI])

        TABW = WPTURN + NWIN
        startTab = sb("startTab", [1, TABW], i32)
        furtherTab = sb("furtherTab", [1, TABW], i32)
        beforeTab = sb("beforeTab", [1, TABW], i32)
        spanTab = sb("spanTab", [1, NBODY + 1, 4], i32)
        grpFirst = sb("grpFirst", [1, NBODY, 8], i32)
        grpFurther = sb("grpFurther", [1, NG], i32)
        grpBefore = sb("grpBefore", [1, NG], i32)
        turnTab = sb("turnTab", [1, NBODY + 1], i32)
        groupTab = sb("groupTab", [1, NBODY], i32)
        iotaLo = sb("iotaLo", [P, P], f16)
        iotaKey = sb("iotaKey", [P, KEYS], f16)
        winBase = sb("winBase", [P, TABW])
        iotaS = sb("iotaS", [P, SW])
        further = sb("further", [P, N // SW + 1])
        dstG = sb("dstG", [P, NG, GJ])

        AREA = 2 * HB * BCOLS
        area = sb("area", [P, AREA])

        def carve(at, cols, dt=f32):
            v = area[:, at:at + cols]
            return v if dt == f32 else v.bitcast(dt)

        ROW = CT * P

        def take_rows(at, dt=f32, t=CT, e=P):
            return carve(at, t * e, dt).rearrange("p (t e) -> p t e", t=t)
        rowDst, rowSrc, rowHi, rowLoI = (take_rows(n * ROW, i32) for n in range(4))
        rowDt, rowNorm, rowW = (take_rows(n * ROW) for n in range(4, 7))
        rowRec = carve(7 * ROW, ROW * REC).rearrange("p (t e f) -> p t e f", t=CT, f=REC)
        rowG = take_rows(12 * ROW, i32, GT, GE)
        rowGf = take_rows(12 * ROW + GT * GE, f32, GT, GE)
        a0 = 12 * ROW + 2 * GT * GE
        wbf = [carve(a0 + q * ROW // 2, ROW // 2, bf16).rearrange("p (t e) -> p t e", t=CT) for q in range(3)]
        a0 += 3 * ROW // 2
        NDIAG = 2 * CT + GT
        diag = carve(a0, NDIAG * P).rearrange("p (k c) -> p k c", k=NDIAG)
        a0 += NDIAG * P
        gath = carve(a0, 2 * WT * P, i32).rearrange("p (k q e) -> p k q e", k=2, q=WT)
        rel = carve(a0 + 2 * WT * P, 2 * WT * P).rearrange("p (k q e) -> p k q e", k=2, q=WT)
        assert a0 + 4 * WT * P <= AREA
        chMinB, chMaxB, m0 = (degB[:, n * NCP:(n + 1) * NCP] for n in range(3))
        m1 = sb("m1", [P, NCP])
        cLess = sb("cLess", [P, NCP])
        cPlus = sb("cPlus", [P, NCP])
        chMM = sb("chMM", [P, 2, CT])
        gMM = sb("gMM", [P, 2, GT])
        winLo = sb("winLo", [P, WT])
        winHi = sb("winHi", [P, WT])
        loHi = sb("loHi", [P, 2, WT])
        rowIdx = sb("rowIdx", [P, 2, WT], i32)
        posLH = sb("posLH", [P, 2, WT])
        colTab = sb("colTab", [P, 2, WT])
        colInt = sb("colInt", [P, WT], i32)
        rowTab = sb("rowTab", [1, 5, NWIN])
        spanF = sb("spanF", [1, 2 * NBLK])
        zrow = sb("zrow", [1, NWIN])
        lamB = sb("lamB", [P, 1])
        lamN = sb("lamN", [P, 1])
        condB = sb("condB", [P, 2])
        mscale = sb("mscale", [P, HI])

        at = 0

        def take(cols, dt=f32):
            nonlocal at
            v = carve(at, cols, dt)
            at += cols
            return v
        hot = [[take(STEP * P // 2, bf16).rearrange("p (j c) -> p j c", j=STEP) for _ in range(4)] for _ in range(SETS)]
        KP = KEYS + 1
        key = [take(STEP * KP // 2, bf16).rearrange("p (j c) -> p j c", j=STEP) for _ in range(SETS)]
        xhot = [take(P // 2, bf16) for _ in range(4)]
        xkey = take(KP // 2, bf16)
        stage = [take(4 * BCOLS).rearrange("p (c m s d) -> p c m s d", c=2, m=2, s=HI) for _ in range(2)]
        ehot = [take(GJ * SW).rearrange("p (j c) -> p j c", j=GJ) for _ in range(ERING)]
        exhot = take(GJ * SW).rearrange("p (j c) -> p j c", j=GJ)
        exrel = take(GJ)
        recs = take(WPTURN * STEP * REC).rearrange("p (w j f) -> p w j f", w=WPTURN, j=STEP)
        keyrel = take(WPTURN * STEP).rearrange("p (w j) -> p w j", w=WPTURN)
        xrec = take(REC)
        xkeyrel = take(1)
        firstAgg = carve(AREA - (NBODY + 2) * FIRST, (NBODY + 2) * FIRST)
        assert at <= AREA - (NBODY + 2) * FIRST
        assert AREA - (NBODY + 2) * FIRST >= HB * BCOLS
        ebuf = sb("ebuf", [P, ERING, GJ, EA])

        at = 0
        strm = [take(HB * BCOLS).rearrange("p (b s d) -> p b s d", b=HB, s=HI) for _ in range(2)]
        assert at <= AREA
        agg0 = [sb(f"agg0{c}", [P, HALF]) for c in range(2)]
        hdeg = [sb(f"hdeg{c}", [P, HALF]) for c in range(2)]
        agg = [sb(f"agg{c}", [P, HALF]) for c in range(2)]
        gate = sb("gate", [P, 4, HALF])
        wnat = ebuf[:, :, :, :].rearrange("p a b c -> p (a b c)")
        unat = wnat[:, 0:2 * F + FE + 2]
        ihnat = wnat[:, 384:384 + 3 * F].rearrange("p (g c) -> p g c", g=3)
        hhnat = wnat[:, 768:768 + 3 * F].rearrange("p (g c) -> p g c", g=3)
        condPart = sb("condPart", [P, 1])
        bnat = sb("bnat", [P, 7])
        bgate = sb("bgate", [P, 4])
        eaw = sb("eaw", [P, F])
        wts = sb("wts", [P, 9, F])

        bank = [pb(f"bank{i}", [P, 512]) for i in range(8)]
        psWin, psE, psX, psFirst = bank[0:4], bank[4:6], bank[6], bank[7]
        psXC, psXW = psX[:, 0:KEYS], psX[:, KEYS:2 * KEYS]
        psP, psM, psR, psZ, psI, psH, psT = bank[0:2], bank[2], bank[3], bank[4], bank[5], bank[6], bank[7]

        const_ready = sem("const_ready")
        pad_ready = sem("pad_ready")
        rows_in = sem("rows_in")
        small_in = sem("small_in")
        xpad_ready = sem("xpad_ready")
        x_in = sem("x_in")
        lam_ready = sem("lam_ready")
        decay_ready = sem("decay_ready")
        int_ready = sem("int_ready")
        part_ready = sem("part_ready")
        key_ready = sem("key_ready")
        recs_ready = sem("recs_ready")
        dst_stored = sem("dst_stored")
        rec_stored = sem("rec_stored")
        idx_ready = sem("idx_ready")
        gathered = sem("gathered")
        scale_ready = sem("scale_ready")
        step_done = sem("step_done")
        diag_ready = sem("diag_ready")
        diag_spread = sem("diag_spread")
        spread_out = sem("spread_out")
        lohi_ready = sem("lohi_ready")
        grp_turned = sem("grp_turned")
        lohi_turned = sem("lohi_turned")
        starts_ready = sem("starts_ready")
        tables_ready = sem("tables_ready")
        var_ready = sem("var_ready")
        std_ready = sem("std_ready")
        norm_ready = sem("norm_ready")
        e_in = [sem(f"e_in{r}") for r in range(ERING)]
        ehot_ready = sem("ehot_ready")
        e_used = sem("e_used")
        e_added = sem("e_added")
        exrel_ready = sem("exrel_ready")
        exhot_ready = sem("exhot_ready")
        ex_done = sem("ex_done")
        ex_added = sem("ex_added")
        hot0_ready = sem("hot0_ready")
        hot1_ready = sem("hot1_ready")
        hot2_ready = sem("hot2_ready")
        hot3_ready = sem("hot3_ready")
        win_done = sem("win_done")
        xhot_ready = sem("xhot_ready")
        xhot_used = sem("xhot_used")
        xrec_in = sem("xrec_in")
        xkeyrel_ready = sem("xkeyrel_ready")
        x_added = sem("x_added")
        rec_in = [sem(f"rec_in{k}") for k in range(QPB)]
        keyrel_ready = sem("keyrel_ready")
        stored = [sem(f"stored{c}") for c in range(2)]
        win_out = sem("win_out")
        turn_ready = sem("turn_ready")
        zeros_ready = sem("zeros_ready")
        first_done = sem("first_done")
        first_out = sem("first_out")
        deg_spread = sem("deg_spread")
        deg_out = sem("deg_out")
        strm_in = [sem(f"strm_in{c}") for c in range(2)]
        prod_done = sem("prod_done")
        prod_out = sem("prod_out")
        hdeg_ready = sem("hdeg_ready")
        msg_done = sem("msg_done")
        agg_ready = sem("agg_ready")
        gates_done = sem("gates_done")
        rz_ready = sem("rz_ready")
        cand_in = sem("cand_in")
        cand_ready = sem("cand_ready")
        gru_step = sem("gru_step")
        h_ready = sem("h_ready")
        w_in = sem("w_in")
        w_prep = sem("w_prep")
        w_turned = sem("w_turned")
        w_ready = sem("w_ready")
        t_done = sem("t_done")
        t_out = sem("t_out")
        res_ready = sem("res_ready")
        out_stored = sem("out_stored")

        AHEAD = 2
        NTB = -(-HI // 4)
        TURN_BANK = (0, 1, 2, 7, 2, 7, 2)

        MOST = NCH * WPTURN + ERING * (N // SW)

        def batch(b):
            return 4 * b, min(4, HI - 4 * b)

        def wait(eng, s, v):
            if not (isinstance(v, int) and v <= 0):
                eng.wait_ge(s, v)

        def entry_regs(eng, name):
            return [eng.alloc_register(f"{name}_entry{n}") for n in range(QUAD)]

        def read4(eng, regs, row, most):
            eng.load(regs, row)
            return [eng.snap(g, min_val=0, max_val=most) for g in regs]

        block = ctx.enter_context(nc.Block())

        @block.sync
        def _(sp):
            sp.wait_ge(pad_ready, 2)
            whole = (CT - 1) * P * P
            k = FULLCH - (CT - 1) * P
            for rows, dram in ((rowDst, dst), (rowSrc, src), (rowDt, dt_in), (rowNorm, norm_in)):
                sp.dma_start(rows[:, 0:CT - 1, :],
                             dram[0:whole].rearrange("(t p e) -> p t e", p=P, e=P)).then_inc(rows_in, 16)
                sp.dma_start(rows[0:k, CT - 1, :],
                             dram[whole:whole + k * P].rearrange("(p e) -> p e", e=P)).then_inc(rows_in, 16)
                sp.dma_start(rows[k:k + 1, CT - 1, 0:E - FULLCH * P],
                             dram[FULLCH * P:E].rearrange("(p e) -> p e", p=1)).then_inc(rows_in, 16)
            k = FULLG - GPT
            sp.dma_start(rowG[0:GPT, 0, :],
                         dst[0:GPT * GE].rearrange("(p e) -> p e", e=GE)).then_inc(rows_in, 16)
            sp.dma_start(rowG[0:k, 1, :],
                         dst[GPT * GE:FULLG * GE].rearrange("(p e) -> p e", e=GE)).then_inc(rows_in, 16)
            sp.dma_start(rowG[k:k + 1, 1, 0:GTAIL],
                         dst[FULLG * GE:E].rearrange("(p e) -> p e", p=1)).then_inc(rows_in, 16)
            sp.dma_start(lamB[:, :], lam.rearrange("(o c) -> o c", o=1).broadcast_to([P, 1])).then_inc(small_in, 16)
            sp.dma_start(condB[:, :], cond.rearrange("(o c) -> o c", o=1).broadcast_to([P, 2])).then_inc(small_in, 16)
            sp.wait_ge(xpad_ready, 1)
            sp.dma_start(x_nat[:, 0:HI - 1, :],
                         x[0:(HI - 1) * P, :].rearrange("(t p) f -> p t f", p=P)).then_inc(x_in, 16)
            sp.dma_start(x_nat[0:N - (HI - 1) * P, HI - 1, :], x[(HI - 1) * P:N, :]).then_inc(x_in, 16)
            sp.wait_ge(rows_in, 15 * 16)
            sp.dma_start(dst_dram.rearrange("(t p) e -> p t e", p=P), rowDst).then_inc(dst_stored, 16)

            def load_group(g, r, partitions=P):
                sp.dma_start(ebuf[0:partitions, r, :, 0:FE],
                             edge_attr[bass.ds(g * GE, partitions * GJ), :].rearrange("(p j) f -> p j f", j=GJ)
                             ).then_inc(e_in[r], 16)

            sp.wait_ge(const_ready, 2)
            for r in range(ERING):
                load_group(r, r)
            sp.wait_ge(recs_ready, 1)
            sp.dma_start(rec_dram.rearrange("(t p e) f -> p t (e f)", p=P, e=P),
                         rowRec.rearrange("p t e f -> p t (e f)")).then_inc(rec_stored, 16)

            regs = entry_regs(sp, "sp")

            def load_records(i, k):
                starts = read4(sp, regs, startTab[0:1, bass.ds(i * WPTURN + (WPTURN + k * QUAD), QUAD)], E + 2 * P)
                for v in range(QUAD):
                    sp.dma_start(recs[:, k * QUAD + v, :, :].rearrange("p j f -> p (j f)"),
                                 rec_dram[bass.ds(starts[v], TAKE), :].rearrange("(p j) f -> p (j f)", j=STEP)
                                 ).then_inc(rec_in[k], 16)

            sp.wait_ge(rec_stored, 16)
            sp.wait_ge(starts_ready, 1)
            for k in range(QPB):
                load_records(0, k)
            sp.wait_ge(tables_ready, 1)

            def further_records(i):
                any_further = sp.value_load(turnTab[0:1, bass.ds(i, 1)], min_val=0, max_val=MOST)
                with sp.If(any_further > 0):
                    span = read4(sp, regs, spanTab[0:1, bass.ds(i, 1), :], WPB)
                    for c in range(2):
                        with sp.If(span[2 * c + 1] > 0):
                            with sp.Fori(span[2 * c], span[2 * c + 1]) as v:
                                w = i * WPTURN + c * WPB + v
                                nx = sp.value_load(furtherTab[0:1, bass.ds(w, 1)], min_val=0, max_val=NCH)
                                with sp.If(nx > 0):
                                    xb = sp.value_load(beforeTab[0:1, bass.ds(w, 1)], min_val=0, max_val=NCH * NWIN)
                                    e0 = sp.value_load(startTab[0:1, bass.ds(w, 1)], min_val=0, max_val=E)
                                    with sp.Fori(0, nx) as n:
                                        sp.wait_ge(xhot_used, xb + n + AHEAD)
                                        at = nc.s_assert_within(e0 + n * P + TAKE, 0, NCP * P - P)
                                        sp.dma_start(xrec, rec_dram[bass.ds(at, P), :]).then_inc(xrec_in, 16)

            def store_turn(i, parity):
                sp.wait_ge(win_out, i * WPTURN + (WPTURN + SETS))
                sp.wait_ge(turn_ready, i + 2)
                b = i * 2 if isinstance(i, int) else nc.s_assert_within(i * 2, 0, NBLK - 2)
                sp.dma_start(mat_dram[bass.ds(b, 2), :, :, :].rearrange("o m p n -> p (o m) n"),
                             stage[parity].rearrange("p c m s d -> p (c m) (s d)")).then_inc(stored[parity], 16)

            def turn(i, parity, partitions, first=None):
                further_records(i)
                for k in range(QPB):
                    if k == 1 and first is not None:
                        with sp.If(first > 0):
                            store_turn(i - 1, 1 - parity)
                    elif k == 1:
                        store_turn(i - 1, 1 - parity)
                    if partitions is None:
                        continue
                    for ready in (hot1_ready, hot2_ready, hot3_ready):
                        sp.wait_ge(ready, i * WPTURN + (k + 1) * QUAD)
                    load_records(i + 1, k)
                    for r in range(2 * k, min(2 * k + 2, ERING)):
                        sp.wait_ge(e_used, i * ERING + (max(r, EARLY) + 1))
                        load_group(i * ERING + ERING + r, r, partitions[r])

            with sp.Fori(0, NBODY // 2 - 1) as ii:
                turn(ii * 2, 0, [P] * ERING, first=ii)
                turn(ii * 2 + 1, 1, [P] * ERING)
            turn(NBODY - 2, 0, [P] * (ERING - 1) + [GTAIL // GJ])
            turn(NBODY - 1, 1, None)
            further_records(NBODY)
            store_turn(NBODY - 1, 1)
            for parity in range(2):
                sp.wait_ge(stored[parity], 16 * (NBODY // 2 + 1))
            sp.wait_ge(win_done, NWIN + SETS)
            sp.wait_ge(e_added, NG + AHEAD)
            sp.wait_ge(first_done, NBODY + 2)

            def load_weights(k):
                sp.dma_start(unat, U_W[k, :, :]).then_inc(w_in, 16)
                sp.dma_start(ihnat, Wih[k, :, :].rearrange("(g a) b -> a g b", a=P)).then_inc(w_in, 16)
                sp.dma_start(hhnat, Whh[k, :, :].rearrange("(g a) b -> a g b", a=P)).then_inc(w_in, 16)
                sp.dma_start(bnat[:, 0:1], U_b[k, :].rearrange("(a o) -> a o", o=1)).then_inc(w_in, 16)
                sp.dma_start(bnat[:, 1:4], bih[k, :].rearrange("(g a) -> a g", a=P),
                             allow_slow_non_contiguous=True).then_inc(w_in, 16)
                sp.dma_start(bnat[:, 4:7], bhh[k, :].rearrange("(g a) -> a g", a=P),
                             allow_slow_non_contiguous=True).then_inc(w_in, 16)

            def load_half(m, j, J, c):
                wait(sp, prod_done, J - 1)
                sp.dma_start(strm[c].rearrange("p b s d -> p b (s d)"),
                             mat_dram[bass.ds(j * HB, HB), m, :, :].rearrange("b p n -> p b n")
                             ).then_inc(strm_in[c], 16)

            load_weights(0)
            sp.wait_ge(w_turned, 3)
            load_weights(1)
            for k in range(1, ROUNDS + 1):
                m = 0 if k < ROUNDS else 1
                for c in range(2):
                    if k == 1 and c == 1:
                        sp.wait_ge(msg_done, NHALF)
                    load_half(m, c, k * NHALF + c, c)
                if k + 1 < ROUNDS:
                    sp.wait_ge(w_turned, 3 * (k + 1))
                    load_weights(k + 1)
                with sp.Fori(1, NSUP) as i:
                    for c in range(2):
                        load_half(m, i * 2 + c, i * 2 + (k * NHALF + c), c)

            for b in range(NTB):
                t0, n = batch(b)
                sp.wait_ge(res_ready, b + 1)
                if (t0 + n) * P <= N:
                    sp.dma_start(out[t0 * P:(t0 + n) * P, :].rearrange("(t p) f -> p t f", p=P),
                                 x_nat[:, t0:t0 + n, :]).then_inc(out_stored, 16)
                else:
                    sp.dma_start(out[t0 * P:N, :], x_nat[0:N - t0 * P, t0, :]).then_inc(out_stored, 16)
            sp.wait_ge(out_stored, 16 * NTB)

        @block.gpsimd
        def _(pool):
            def iota(out_ap, pattern, base=0, channel=0):
                return nc.gpsimd.iota(out_ap, pattern=pattern, base=base, channel_multiplier=channel,
                                      allow_small_or_imprecise_dtypes=True)

            nc.gpsimd.memset(x_nat[:, HI - 1, :], 0.0).then_inc(xpad_ready, 1)
            nc.gpsimd.memset(ident[:, :], 0.0).then_inc(const_ready, 1)
            nc.gpsimd.memset(ebuf[:, :, :, :], 1.0).then_inc(const_ready, 1)
            pool.wait_ge(const_ready, 1)
            nc.gpsimd.memset(ones[:, :], 1.0)
            nc.gpsimd.affine_select(out=ident[:, :], in_=ident[:, :], compare_op=ALU.not_equal, fill=1.0, base=0,
                                    pattern=[[-1, P]], channel_multiplier=1).then_inc(const_ready, 1)
            iota(iotaLo[:, :], [[1, P]])
            iota(iotaKey[:, :], [[1, KEYS]])
            iota(iotaS[:, :], [[1, SW]])
            iota(further[:, :], [[-SW, N // SW + 1]], base=-SW)
            iota(winLo[:, :], [[WPT * WD, WT]], channel=WD)
            iota(winHi[:, :], [[WPT * WD, WT]], base=WD - 1, channel=WD)
            iota(cLess[:, :], [[-1, NCP]], base=int(BIG))
            iota(cPlus[:, :], [[1, NCP]], base=1)
            nc.gpsimd.memset(zrow[:, :], 0.0).then_inc(const_ready, 1)
            iota(winBase[:, :], [[KEYS, TABW]], base=-KEYS * WPTURN)
            nc.gpsimd.memset(sumE[:, :], 0.0)
            nc.gpsimd.memset(eaw[:, :], 0.0).then_inc(const_ready, 1)

            pool.wait_ge(dst_stored, 16)
            pool.wait_ge(idx_ready, 1)
            for k in range(2):
                for q in range(WT):
                    nc.gpsimd.indirect_dma_start(
                        out=gath[0:WPT, k, q, :], out_offset=None, in_=dst_dram[:, :],
                        in_offset=bass.IndirectOffsetOnAxis(ap=rowIdx[0:WPT, k, q:q + 1], axis=0)).then_inc(gathered, 16)

            pool.wait_ge(tables_ready, 1)
            pool.wait_ge(rec_stored, 16)
            nc.gpsimd.memset(stage[1][:, :, 0, :, :], 0.0).then_inc(zeros_ready, 1)

            def per_row(w, j0, j1, f):
                return recs[:, w, j0:j1, f:f + 1].broadcast_to([P, j1 - j0, P])

            with pool.Fori(0, NBODY) as i:
                for u in range(WPTURN):
                    w, s = i * WPTURN + u, u % SETS
                    pool.wait_ge(hot0_ready, w + 1)
                    nc.gpsimd.tensor_tensor(hot[s][1][:, 0:1, :], hot[s][0][:, 0:1, :], per_row(u, 0, 1, 2), ALU.mult)
                    nc.gpsimd.tensor_tensor(hot[s][3], hot[s][0], per_row(u, 0, STEP, 4),
                                            ALU.mult).then_inc(hot3_ready, 1)

        @block.scalar
        def _(act):
            act.sem_inc(win_out, SETS)
            for parity in range(2):
                act.sem_inc(stored[parity], 16)
            act.sem_inc(rz_ready, AHEAD)
            act.wait_ge(lam_ready, 2)
            act.wait_ge(rows_in, 15 * 16)
            nc.scalar.activation(rowW, rowDt, ACT.Exp, scale=lamN[:, 0:1]).then_inc(decay_ready, 1)
            act.wait_ge(int_ready, 1)
            nc.scalar.copy(rowRec[:, :, :, 0], rowLoI)
            for q in range(3):
                act.wait_ge(part_ready, q + 1)
                last = nc.scalar.copy(rowRec[:, :, :, 2 + q], wbf[q])
            act.wait_ge(key_ready, 1)
            last.then_inc(recs_ready, 1)
            act.wait_ge(var_ready, 1)
            nc.scalar.activation(rstd[:, :], mv[:, :, 1], ACT.Sqrt).then_inc(std_ready, 1)

            def norm_apply(n):
                act.wait_ge(scale_ready, n)
                for t in range(HI):
                    nc.scalar.activation(h_nat[:, t, :], x_nat[:, t, :], ACT.Relu, bias=mscale[:, t:t + 1],
                                         scale=rstd[:, t:t + 1]).then_inc(norm_ready, 1)

            norm_apply(1)
            for b in range(NTB):
                t0, n = batch(b)
                act.wait_ge(t_done, b + 1)
                nc.scalar.copy(hT[:, t0 * P:(t0 + n) * P], bank[6 + b % 2][:, 0:n * P]).then_inc(t_out, 1)

            def window_out(i, parity, u):
                w, s, d = i * WPTURN + u, u % SETS, u % WPB * WD
                if u == 0:
                    act.wait_ge(stored[parity], i * 8 + (16 - parity * 8))
                    act.wait_ge(first_done, i + 1)
                act.wait_ge(win_done, w + (1 + SETS))
                nc.scalar.copy(stage[parity][:, u // WPB, :, :, d:d + WD],
                               psWin[s][:, 0:2 * KEYS].rearrange("p (m d s) -> p m s d", m=2, s=HI)).then_inc(win_out, 1)

            def first_sums_out(i):
                act.wait_ge(first_done, i + 1)
                nc.scalar.copy(firstAgg[:, bass.ds(i * FIRST, FIRST)], psFirst[:, 0:FIRST]).then_inc(first_out, 1)

            def turn(i, parity, first=None):
                for u in range(WPTURN):
                    w, s = i * WPTURN + u, u % SETS
                    act.wait_ge(hot0_ready, w + 1)
                    for j in range(STEP):
                        last = nc.scalar.activation(hot[s][2][:, j, :], hot[s][0][:, j, :], ACT.Copy,
                                                    scale=recs[:, u, j, 3:4])
                    if u in ACT_TOO:
                        last = nc.scalar.activation(hot[s][1][:, 1, :], hot[s][0][:, 1, :], ACT.Copy,
                                                    scale=recs[:, u, 1, 2:3])
                    last.then_inc(hot2_ready, 1)
                    if u >= 2:
                        window_out(i, parity, u - 2)
                        if u == 3:
                            first_sums_out(i)
                    elif u == 1 and first is not None:
                        with act.If(first > 0):
                            for before in (WPTURN - 2, WPTURN - 1):
                                window_out(i - 1, 1 - parity, before)
                    elif u == 1:
                        for before in (WPTURN - 2, WPTURN - 1):
                            window_out(i - 1, 1 - parity, before)

            act.wait_ge(tables_ready, 1)
            with act.Fori(0, NBODY // 2) as ii:
                turn(ii * 2, 0, first=ii)
                turn(ii * 2 + 1, 1)
            for before in (WPTURN - 2, WPTURN - 1):
                window_out(NBODY - 1, 1, before)
            for i in range(NBODY, NBODY + 2):
                first_sums_out(i)

            for j in range(NHALF):
                act.wait_ge(deg_spread, j + 1)
                nc.scalar.copy(degB[:, j * HALF:(j + 1) * HALF], bank[6 + j % 2][:, 0:HALF]).then_inc(deg_out, 1)

            def product_out(J, c):
                act.wait_ge(prod_done, J + 1)
                nc.scalar.copy(agg0[c][:, :], psP[c][:, 0:HALF]).then_inc(prod_out, 1)

            def message_out(J, c):
                act.wait_ge(msg_done, J + 1)
                nc.scalar.copy(agg[c][:, :], psM[:, 0:HALF]).then_inc(agg_ready, 1)

            def gates(J, c):
                act.wait_ge(gates_done, J + 1)
                act.wait_ge(h_ready, J + AHEAD)
                nc.scalar.activation(gate[:, 0, :], psR[:, 0:HALF], ACT.Sigmoid, bias=bgate[:, 0:1])
                nc.scalar.activation(gate[:, 1, :], psZ[:, 0:HALF], ACT.Sigmoid, bias=bgate[:, 1:2]).then_inc(rz_ready, 1)
                act.wait_ge(cand_in, J + 1 + AHEAD)
                nc.scalar.activation(gate[:, 2, :], gate[:, 3, :], ACT.Tanh, bias=bgate[:, 2:3]).then_inc(cand_ready, 1)

            for k in range(ROUNDS):
                for b in range(3):
                    act.wait_ge(w_turned, 3 * k + b + 1)
                    nc.scalar.copy(wts[:, 3 * b:3 * b + 3, :],
                                   bank[3 + b][:, 0:3 * F].rearrange("p (g c) -> p g c", g=3)).then_inc(w_ready, 1)
                J = k * NHALF
                if k == 0:
                    act.sem_inc(prod_out, NHALF)
                else:
                    product_out(J, 0)
                    product_out(J + 1, 1)
                message_out(J, 0)
                with act.Fori(1, NSUP) as i:
                    for c in range(2):
                        if k > 0:
                            product_out(i * 2 + (J + c), c)
                        message_out(i * 2 + (J + c - 1), 1 - c)
                        gates(i * 2 + (J + c - 2), c)
                J += NHALF
                message_out(J - 1, 1)
                gates(J - 2, 0)
                gates(J - 1, 1)
                if k < ROUNDS - 1:
                    for b in range(NTB):
                        t0, n = batch(b)
                        act.wait_ge(t_done, NTB * (k + 1) + b + 1)
                        nc.scalar.copy(h_nat[:, t0:t0 + n, :],
                                       bank[TURN_BANK[b]][:, 0:n * P].rearrange("p (t f) -> p t f", f=F)
                                       ).then_inc(t_out, 1)
            act.wait_ge(var_ready, 2)
            nc.scalar.activation(rstd[:, :], mv[:, :, 1], ACT.Sqrt).then_inc(std_ready, 1)
            norm_apply(2)
            with act.Fori(0, NSUP) as i:
                for c in range(2):
                    act.wait_ge(prod_done, i * 2 + (ROUNDS * NHALF + c + 1))
                    nc.scalar.copy(hT[:, bass.ds(i * (2 * HALF) + c * HALF, HALF)], psP[c][:, 0:HALF]).then_inc(prod_out, 1)

        @block.vector
        def _(dve):
            steps = [0]

            def link(ins):
                steps[0] += 1
                ins.then_inc(step_done, 1)
                dve.wait_ge(step_done, steps[0])

            dve.sem_inc(e_added, AHEAD)
            dve.sem_inc(ex_added, AHEAD)
            dve.sem_inc(h_ready, AHEAD)
            dve.sem_inc(cand_in, AHEAD)
            nc.vector.memset(rowDst, NODST)
            nc.vector.memset(rowSrc, 0)
            nc.vector.memset(rowG, NODST).then_inc(pad_ready, 1)
            nc.vector.memset(rowDt, 0.0)
            nc.vector.memset(rowNorm, 0.0).then_inc(pad_ready, 1)
            dve.wait_ge(small_in, 32)
            nc.vector.tensor_scalar(lamN[:, :], lamB[:, :], 0.0, 1e-4, ALU.max, ALU.add).then_inc(lam_ready, 1)
            dve.wait_ge(lam_ready, 1)
            nc.vector.tensor_scalar(lamN[:, :], lamN[:, :], -1.0, None, ALU.mult).then_inc(lam_ready, 1)

            dve.wait_ge(rows_in, 15 * 16)
            nc.vector.tensor_reduce(chMM[:, 0, :], rowDst, AX.X, ALU.min)
            nc.vector.tensor_reduce(chMM[:, 1, :], rowDst, AX.X, ALU.max)
            nc.vector.tensor_single_scalar(rowLoI, rowSrc, P - 1, ALU.bitwise_and).then_inc(int_ready, 1)
            dve.wait_ge(int_ready, 1)
            dve.wait_ge(const_ready, 3)

            def diagonal(n, value, size):
                nc.vector.tensor_scalar(diag[0:size, n, 0:size], ident[0:size, 0:size], value, None,
                                        ALU.mult).then_inc(diag_ready, 1)

            for k in range(2):
                for t in range(CT):
                    diagonal(k * CT + t, chMM[:, k, t:t + 1], P)
            for k, dest in enumerate((chMinB, chMaxB)):
                dve.wait_ge(diag_spread, CT * (k + 1))
                nc.vector.tensor_copy(dest[:, 0:512], bank[2 * k][:, :])
                nc.vector.tensor_copy(dest[:, 512:NCP], bank[2 * k + 1][:, 0:NCP - 512]).then_inc(spread_out, 1)
            dve.wait_ge(spread_out, 2)
            dve.wait_ge(const_ready, 4)
            W, C = slice(0, WPT), slice(0, NCH)
            for q in range(WT):
                link(nc.vector.tensor_scalar(m0[W, C], chMinB[W, C], winHi[W, q:q + 1], None, ALU.is_le))
                link(nc.vector.scalar_tensor_tensor(m1[W, C], chMaxB[W, C], winLo[W, q:q + 1], m0[W, C],
                                                    ALU.is_ge, ALU.mult))
                for k, factor in enumerate((cLess, cPlus)):
                    ins = nc.vector.tensor_tensor_reduce(out=m0[W, C], in0=m1[W, C], in1=factor[W, C], scale=1.0,
                                                         scalar=0.0, op0=ALU.mult, op1=ALU.max,
                                                         accum_out=loHi[W, k, q:q + 1])
                    link(ins)
            link(nc.vector.tensor_scalar(loHi[W, 0, :], loHi[W, 0, :], -1.0, BIG, ALU.mult, ALU.add))
            link(nc.vector.tensor_scalar(loHi[W, 0, :], loHi[W, 0, :], float(NCH), None, ALU.min))
            link(nc.vector.tensor_scalar(loHi[W, 1, :], loHi[W, 1, :], -1.0, 0.0, ALU.add, ALU.max))
            nc.vector.tensor_copy(rowIdx[W, :, :], loHi[W, :, :]).then_inc(idx_ready, 1)

            dve.wait_ge(decay_ready, 1)
            nc.vector.tensor_single_scalar(rowHi, rowSrc, 7, ALU.arith_shift_right)
            link(nc.vector.tensor_tensor(rowW, rowW, rowNorm, ALU.mult))
            for q in range(3):
                nc.vector.tensor_copy(wbf[q], rowW).then_inc(part_ready, 1)
                if q == 0:
                    nc.vector.scalar_tensor_tensor(rowRec[:, :, :, 1], rowDst, float(HI), rowHi, ALU.mult,
                                                   ALU.add).then_inc(key_ready, 1)
                if q < 2:
                    dve.wait_ge(part_ready, q + 1)
                    link(nc.vector.tensor_tensor(rowW, rowW, wbf[q], ALU.subtract))
            def tile_stats(t0, t1):
                for t in range(t0, t1):
                    last = nc.vector.bn_stats(stats[:, t, :], x_nat[:, t, :])
                return last

            def norm_stats():
                for t in range(HI):
                    last = nc.vector.bn_aggr(mv[:, t, :], stats[:, t, :])
                link(last)
                nc.vector.tensor_scalar(mv[:, :, 1], mv[:, :, 1], EPS, None, ALU.add).then_inc(var_ready, 1)

            def norm_scale(n):
                dve.wait_ge(std_ready, n)
                link(nc.vector.reciprocal(rstd[:, :], rstd[:, :]))
                nc.vector.scalar_tensor_tensor(mscale[:, :], mv[:, :, 0], -1.0, rstd[:, :], ALU.mult,
                                               ALU.mult).then_inc(scale_ready, 1)

            dve.wait_ge(x_in, 32)
            link(tile_stats(0, HI))
            norm_stats()
            nc.vector.tensor_reduce(gMM[0:GPT, 0, :], rowG[0:GPT], AX.X, ALU.min)
            nc.vector.tensor_reduce(gMM[0:GPT, 1, :], rowG[0:GPT], AX.X, ALU.max)
            link(nc.vector.tensor_copy(rowGf[0:GPT], rowG[0:GPT]))
            link(nc.vector.tensor_scalar(gMM[0:GPT], gMM[0:GPT], float(N - 1), None, ALU.min))
            for t in range(GT):
                diagonal(2 * CT + t, gMM[0:GPT, 0, t:t + 1], GPT)

            dve.wait_ge(grp_turned, 1)
            link(nc.vector.tensor_copy(dstG[:, :, 0], bank[4][:, 0:NG]))
            for j in range(GJ - 1, -1, -1):
                nc.vector.tensor_tensor(dstG[:, :, j], bank[5 + j // 2][:, (j % 2) * NG:(j % 2 + 1) * NG],
                                        dstG[:, :, 0], ALU.subtract)

            norm_scale(1)

            dve.wait_ge(gathered, 2 * WT * 16)
            lows = winLo[W, :].rearrange("p (q o) -> p q o", o=1).broadcast_to([WPT, WT, P])
            for k in range(2):
                last = nc.vector.tensor_tensor(rel[W, k, :, :], gath[W, k, :, :], lows, ALU.subtract)
            link(last)
            inside = gath.bitcast(f32)
            link(nc.vector.tensor_scalar(inside[W], rel[W], 0.0, None, ALU.is_ge))
            link(nc.vector.scalar_tensor_tensor(inside[W], rel[W], float(WD - 1), inside[W], ALU.is_le, ALU.mult))
            for k, factor in enumerate((cLess, cPlus)):
                f = factor[W, 0:P].rearrange("p (o e) -> p o e", o=1).broadcast_to([WPT, WT, P])
                last = nc.vector.tensor_tensor(rel[W, k, :, :], inside[W, k, :, :], f, ALU.mult)
            link(last)
            link(nc.vector.tensor_reduce(posLH[W, :, :], rel[W], AX.X, ALU.max))
            link(nc.vector.tensor_scalar(posLH[W, 0, :], posLH[W, 0, :], -1.0, BIG, ALU.mult, ALU.add))
            link(nc.vector.tensor_scalar(posLH[W, 0, :], posLH[W, 0, :], float(P), None, ALU.min))
            link(nc.vector.scalar_tensor_tensor(posLH[W, :, :], loHi[W, :, :], float(P), posLH[W, :, :],
                                                ALU.mult, ALU.add))
            nc.vector.tensor_copy(colTab[W, 0, :], posLH[W, 0, :])
            link(nc.vector.tensor_tensor(posLH[W, 1, :], posLH[W, 1, :], posLH[W, 0, :], ALU.subtract))
            link(nc.vector.tensor_scalar(posLH[W, 1, :], posLH[W, 1, :], float(P - 1 - TAKE), 0.0, ALU.add, ALU.max))
            link(nc.vector.tensor_copy(colInt[W, :], posLH[W, 1, :]))
            link(nc.vector.tensor_single_scalar(colInt[W, :], colInt[W, :], 7, ALU.arith_shift_right))
            nc.vector.tensor_copy(colTab[W, 1, :], colInt[W, :]).then_inc(lohi_ready, 1)

            dve.wait_ge(lohi_turned, 1)
            R = [rowTab[:, n, :] for n in range(5)]
            G = [rowTab[:, n, 0:NG] for n in (4, 1, 2, 3)]
            link(nc.vector.memset(startTab[:, 0:WPTURN], 0))
            nc.vector.tensor_copy(startTab[:, WPTURN:TABW], bank[0][0:1, 0:NWIN]).then_inc(starts_ready, 1)
            nc.vector.tensor_copy(R[1], bank[1][0:1, 0:NWIN])
            nc.vector.tensor_copy(G[0], bank[2][0:1, 0:NG])
            link(nc.vector.tensor_copy(R[3][:, 0:NG], bank[2][0:1, NG:2 * NG]))
            nc.vector.tensor_copy(furtherTab[:, WPTURN:TABW], R[1])
            winSum, turnSum = R[3][:, NG:NG + NBODY], R[3][:, NG + NBODY:NG + 2 * NBODY + 1]
            for tab in (furtherTab, beforeTab):
                nc.vector.memset(tab[:, 0:WPTURN], 0)
            nc.vector.memset(turnSum[:, NBODY:NBODY + 1], 0.0)
            nc.vector.tensor_reduce(winSum, R[1].rearrange("p (i w) -> p i w", w=WPTURN), AX.X, ALU.add)
            link(nc.vector.tensor_tensor_scan(R[2], R[1], zrow[:, :], 0.0, ALU.add, ALU.add))
            some = rowTab[:, 0, :].rearrange("p (b v) -> p b v", v=WPB)
            spans = spanF[:, :].rearrange("p (b k) -> p b k", k=2)
            for k, factor in enumerate((cLess, cPlus)):
                f = factor[0:1, 0:WPB].rearrange("p (o v) -> p o v", o=1).broadcast_to([1, NBLK, WPB])
                link(nc.vector.scalar_tensor_tensor(some, R[1].rearrange("p (b v) -> p b v", v=WPB), 0.0, f,
                                                    ALU.is_gt, ALU.mult))
                link(nc.vector.tensor_reduce(spans[:, :, k], some, AX.X, ALU.max))
            link(nc.vector.tensor_scalar(spans[:, :, 0], spans[:, :, 0], -1.0, BIG, ALU.mult, ALU.add))
            link(nc.vector.tensor_tensor(spans[:, :, 0], spans[:, :, 0], spans[:, :, 1], ALU.min))
            nc.vector.memset(spanTab[:, 0:1, :], 0)
            nc.vector.tensor_copy(spanTab[:, 1:NBODY + 1, :], spanF[:, :].rearrange("p (i k) -> p i k", k=4))
            link(nc.vector.tensor_tensor(beforeTab[:, WPTURN:TABW], R[2], R[1], ALU.subtract))
            nc.vector.memset(grpFirst[:, :, ERING:8], 0)
            nc.vector.tensor_copy(grpFirst[:, :, 0:ERING], G[0].rearrange("p (b r) -> p b r", r=ERING))
            link(nc.vector.tensor_tensor(grpFurther[:, :], G[3], G[0], ALU.subtract))
            link(nc.vector.tensor_single_scalar(grpFurther[:, :], grpFurther[:, :], 5, ALU.arith_shift_right))
            link(nc.vector.tensor_copy(G[1], grpFurther[:, :]))
            nc.vector.tensor_reduce(turnSum[:, 0:NBODY], G[1].rearrange("p (b r) -> p b r", r=ERING), AX.X, ALU.add)
            link(nc.vector.tensor_tensor_scan(G[2], G[1], zrow[:, 0:NG], 0.0, ALU.add, ALU.add))
            link(nc.vector.tensor_copy(groupTab[:, :], turnSum[:, 0:NBODY]))
            link(nc.vector.tensor_tensor(turnSum[:, 1:NBODY + 1], turnSum[:, 1:NBODY + 1], winSum, ALU.add))
            nc.vector.tensor_copy(turnTab[:, :], turnSum)
            nc.vector.tensor_tensor(grpBefore[:, :], G[2], G[1], ALU.subtract).then_inc(tables_ready, 1)

            def rows_of(ap):
                return ap.rearrange("p (j o) -> p j o", o=1).broadcast_to([P, GJ, SW])

            along = iotaS[:, :].rearrange("p (o c) -> p o c", o=1).broadcast_to([P, GJ, SW])

            def quad_keys(i, k):
                dve.wait_ge(rec_in[k], i * (QUAD * 16) + QUAD * 16)
                sl = slice(k * QUAD, (k + 1) * QUAD)
                base = winBase[:, bass.ds(i * WPTURN + (WPTURN + k * QUAD), QUAD)]
                nc.vector.tensor_tensor(keyrel[:, sl, :], recs[:, sl, :, 1],
                                        base.rearrange("p (w o) -> p w o", o=1).broadcast_to([P, QUAD, STEP]),
                                        ALU.subtract).then_inc(keyrel_ready, 1)
                dve.wait_ge(keyrel_ready, i * QPB + (k + 1))

            def window_hot(i, u):
                w, s = i * WPTURN + u, u % SETS
                dve.wait_ge(win_done, w + 1)
                for j in range(STEP):
                    last = nc.vector.tensor_scalar(hot[s][0][:, j, :], iotaLo[:, :], recs[:, u, j, 0:1], None,
                                                   ALU.is_equal)
                last.then_inc(hot0_ready, 1)
                if u not in ACT_TOO:
                    nc.vector.tensor_scalar(hot[s][1][:, 1, :], iotaLo[:, :], recs[:, u, 1, 0:1],
                                            recs[:, u, 1, 2:3], ALU.is_equal, ALU.mult)
                for j in range(STEP):
                    last = nc.vector.tensor_scalar(key[s][:, j, 0:KEYS], iotaKey[:, :], keyrel[:, u, j:j + 1], None,
                                                   ALU.is_equal)
                last.then_inc(hot1_ready, 1)

            def further_edges(i, parity):
                span = read4(dve, span_regs, spanTab[0:1, bass.ds(i, 1), :], WPB)
                for c in range(2):
                    with dve.If(span[2 * c + 1] > 0):
                        with dve.Fori(span[2 * c], span[2 * c + 1]) as v:
                            w = i * WPTURN + c * WPB + v
                            nx = dve.value_load(furtherTab[0:1, bass.ds(w, 1)], min_val=0, max_val=NCH)
                            with dve.If(nx > 0):
                                xb = dve.value_load(beforeTab[0:1, bass.ds(w, 1)], min_val=0, max_val=NCH * NWIN)
                                with dve.Fori(0, nx) as n:
                                    dve.wait_ge(xrec_in, (xb + n) * 16 + 16)
                                    nc.vector.tensor_tensor(xkeyrel, xrec[:, 1:2], winBase[:, bass.ds(w, 1)],
                                                            ALU.subtract).then_inc(xkeyrel_ready, 1)
                                    dve.wait_ge(xkeyrel_ready, xb + n + 1)
                                    nc.vector.tensor_scalar(xhot[0], iotaLo[:, :], xrec[:, 0:1], None, ALU.is_equal)
                                    for q in range(3):
                                        nc.vector.tensor_scalar(xhot[q + 1], iotaLo[:, :], xrec[:, 0:1],
                                                                xrec[:, 2 + q:3 + q], ALU.is_equal, ALU.mult)
                                    nc.vector.tensor_scalar(xkey[:, 0:KEYS], iotaKey[:, :], xkeyrel, None,
                                                            ALU.is_equal).then_inc(xhot_ready, 1)
                                    dve.wait_ge(xhot_used, xb + n + 1 + AHEAD)
                                    dve.wait_ge(win_out, i * WPTURN + SETS)
                                    for m, ps in enumerate((psXC, psXW)):
                                        part = stage[parity][:, c, m, :, bass.ds(v * WD, WD)]
                                        last = nc.vector.tensor_tensor(
                                            part, part, ps[:, 0:KEYS].rearrange("p (d s) -> p s d", s=HI), ALU.add)
                                    last.then_inc(x_added, 1)
                                    dve.wait_ge(x_added, xb + n + 1)

            def group_rel(g):
                return dstG[:, bass.ds(g, 1), :].rearrange("p o j -> p (o j)")

            def further_groups(i):
                for r in range(ERING):
                    g = i * ERING + r
                    nx = dve.value_load(grpFurther[0:1, bass.ds(g, 1)], min_val=0, max_val=N // SW)
                    with dve.If(nx > 0):
                        xb = dve.value_load(grpBefore[0:1, bass.ds(g, 1)], min_val=0, max_val=NG * (N // SW))
                        d0 = dve.value_load(grpFirst[0:1, bass.ds(i, 1), r:r + 1], min_val=0, max_val=N - 1)
                        with dve.Fori(0, nx) as n:
                            nc.vector.tensor_scalar(exrel, group_rel(g), further[:, bass.ds(n, 1)], None,
                                                    ALU.add).then_inc(exrel_ready, 1)
                            dve.wait_ge(exrel_ready, xb + n + 1)
                            nc.vector.tensor_tensor(exhot, along, rows_of(exrel),
                                                    ALU.is_equal).then_inc(exhot_ready, 1)
                            dve.wait_ge(ex_done, xb + n + 1)
                            dve.wait_ge(e_added, i * ERING + (1 + AHEAD))
                            dve.wait_ge(ex_added, xb + n + AHEAD)
                            cols = bass.ds(nc.s_assert_within(d0 + n * SW + SW, 0, N - 1), SW)
                            nc.vector.tensor_tensor(sumE[:, cols], sumE[:, cols], psXC[0:EA, 0:SW],
                                                    ALU.add).then_inc(ex_added, 1)
                            dve.wait_ge(ex_added, xb + n + 1 + AHEAD)

            def look_further(i):
                return dve.value_load(turnTab[0:1, bass.ds(i, 1)], min_val=0, max_val=MOST)

            def further_work(i, parity, any_further):
                with dve.If(any_further > 0):
                    further_edges(i, 1 - parity)
                    if not isinstance(i, int):
                        groups_further = dve.value_load(groupTab[0:1, bass.ds(i, 1)], min_val=0, max_val=MOST)
                        with dve.If(groups_further > 0):
                            further_groups(i)
                dve.sem_inc(turn_ready, 1)

            def group_hot(i, r):
                nc.vector.tensor_tensor(ehot[r], along, rows_of(group_rel(i * ERING + r)),
                                        ALU.is_equal).then_inc(ehot_ready, 1)

            def group_add(i, r, d0):
                g = i * ERING + r
                dve.wait_ge(e_used, g + 1)
                dve.wait_ge(e_added, g + AHEAD)
                nc.vector.tensor_tensor(sumE[:, bass.ds(d0, SW)], sumE[:, bass.ds(d0, SW)],
                                        psE[r % 2][0:EA, r // 2 * SW:(r // 2 + 1) * SW], ALU.add).then_inc(e_added, 1)

            regs, held, span_regs = entry_regs(dve, "dve"), {}, entry_regs(dve, "dve_span")
            dve.wait_ge(tables_ready, 1)
            dve.wait_ge(const_ready, 5)
            dve.wait_ge(rec_stored, 16)
            def turn(i, parity):
                for u in range(WPTURN):
                    if u % QUAD == 0:
                        quad_keys(i, u // QUAD)
                    if u % 8 == 1:
                        at = u // 8 * 4
                        first = read4(dve, regs, grpFirst[0:1, bass.ds(i, 1), at:at + 4], N - 1)
                        held.update({at + n: first[n] for n in range(4)})
                    window_hot(i, u)
                    if u == 1:
                        any_further = look_further(i)
                    if u in GROUP_AT:
                        group_hot(i, GROUP_AT.index(u))
                    if u - 2 in GROUP_AT:
                        r = GROUP_AT.index(u - 2)
                        group_add(i, r, held[r])
                    if u == FURTHER_AT:
                        further_work(i, parity, any_further)

            with dve.Fori(0, NBODY // 2) as ii:
                turn(ii * 2, 0)
                turn(ii * 2 + 1, 1)
            further_work(NBODY, 0, look_further(NBODY))

            def weights(k):
                dve.wait_ge(w_in, 16 * 6 * (k + 1))
                nc.vector.tensor_copy(eaw[:, 0:FE], unat[:, 2 * F:2 * F + FE])
                nc.vector.tensor_tensor(bgate[:, 0:2], bnat[:, 1:3], bnat[:, 4:6], ALU.add)
                nc.vector.tensor_copy(bgate[:, 2:4], bnat[:, 3:7:3])
                link(nc.vector.scalar_tensor_tensor(condPart[:, :], condB[:, 0:1], unat[:, 2 * F + FE:2 * F + FE + 1],
                                                    bnat[:, 0:1], ALU.mult, ALU.add))
                nc.vector.scalar_tensor_tensor(eaw[:, FE:FE + 1], condB[:, 1:2], unat[:, 2 * F + FE + 1:2 * F + FE + 2],
                                               condPart[:, :], ALU.mult, ALU.add).then_inc(w_prep, 1)

            def times_degree(j, J, c):
                wait(dve, msg_done, J - 1)
                cols = bass.ds(j * HALF, HALF)
                nc.vector.tensor_tensor(hdeg[c][:, :], hT[:, cols], degB[:, cols], ALU.mult).then_inc(hdeg_ready, 1)

            def update(j, J):
                cols = bass.ds(j * HALF, HALF)
                dve.wait_ge(rz_ready, J + 1 + AHEAD)
                nc.vector.scalar_tensor_tensor(gate[:, 3, :], psH[:, 0:HALF], bgate[:, 3:4], gate[:, 0, :],
                                               ALU.add, ALU.mult).then_inc(gru_step, 1)
                dve.wait_ge(gru_step, J * 3 + 1)
                nc.vector.tensor_tensor(gate[:, 3, :], gate[:, 3, :], psI[:, 0:HALF], ALU.add).then_inc(cand_in, 1)
                dve.wait_ge(cand_ready, J + 1)
                nc.vector.tensor_tensor(gate[:, 3, :], hT[:, cols], gate[:, 2, :], ALU.subtract).then_inc(gru_step, 1)
                dve.wait_ge(gru_step, J * 3 + 2)
                nc.vector.tensor_tensor(gate[:, 3, :], gate[:, 3, :], gate[:, 1, :], ALU.mult).then_inc(gru_step, 1)
                dve.wait_ge(gru_step, J * 3 + 3)
                nc.vector.tensor_tensor(hT[:, cols], gate[:, 2, :], gate[:, 3, :], ALU.add).then_inc(h_ready, 1)

            dve.wait_ge(deg_out, NHALF)
            for k in range(ROUNDS):
                weights(k)
                J = k * NHALF
                dve.wait_ge(h_ready, J + AHEAD)
                times_degree(0, J, 0)
                times_degree(1, J + 1, 1)
                with dve.Fori(1, NSUP) as i:
                    for c in range(2):
                        times_degree(i * 2 + c, i * 2 + (J + c), c)
                        update(i * 2 + (c - 2), i * 2 + (J + c - 2))
                J += NHALF
                update(NHALF - 2, J - 2)
                update(NHALF - 1, J - 1)

            for b in range(NTB):
                t0, n = batch(b)
                dve.wait_ge(t_done, NTB * (ROUNDS + 0) + b + 1)
                nc.vector.tensor_tensor(x_nat[:, t0:t0 + n, :], x_nat[:, t0:t0 + n, :],
                                        bank[TURN_BANK[b]][:, 0:n * P].rearrange("p (t f) -> p t f", f=F),
                                        ALU.add).then_inc(t_out, 1)
                if b > 0:
                    dve.wait_ge(t_out, NTB * ROUNDS + b)
                    tile_stats(4 * (b - 1), 4 * b)
            dve.wait_ge(t_out, NTB * (ROUNDS + 1))
            link(tile_stats(4 * (NTB - 1), HI))
            norm_stats()
            norm_scale(2)
            for b in range(NTB):
                t0, n = batch(b)
                dve.wait_ge(t_done, NTB * (ROUNDS + 1) + b + 1)
                nc.vector.tensor_tensor(x_nat[:, t0:t0 + n, :], x_nat[:, t0:t0 + n, :],
                                        bank[6 + b % 2][:, 0:n * P].rearrange("p (t f) -> p t f", f=F),
                                        ALU.add).then_inc(res_ready, 1)

        @block.tensor
        def _(pe):
            pe.sem_inc(win_done, SETS)
            pe.sem_inc(xhot_used, AHEAD)
            pe.wait_ge(const_ready, 3)
            for k in range(2):
                for t in range(CT):
                    n = k * CT + t
                    pe.wait_ge(diag_ready, n + 1)
                    nc.tensor.matmul(bank[2 * k + t // 4][:, t % 4 * P:(t % 4 + 1) * P], ones[:, :],
                                     diag[:, n, :], start=True, stop=True).then_inc(diag_spread, 1)
            for t in range(GT):
                pe.wait_ge(diag_ready, 2 * CT + t + 1)
                nc.tensor.matmul(bank[4][:, t * GPT:(t + 1) * GPT], ones[0:GPT, :],
                                 diag[0:GPT, 2 * CT + t, 0:GPT], start=True, stop=True).then_inc(diag_spread, 1)
            for j in range(GJ):
                for t in range(GT):
                    last = nc.tensor.transpose(bank[5 + j // 2][:, (j % 2) * NG + t * GPT:(j % 2) * NG + (t + 1) * GPT],
                                               rowGf[0:GPT, t, bass.ds(j, P, GJ)], ident[0:GPT, 0:GPT])
            last.then_inc(grp_turned, 1)
            pe.wait_ge(lohi_ready, 1)
            for k in range(2):
                for q in range(WT):
                    nc.tensor.matmul(bank[k][0:1, q * WPT:(q + 1) * WPT], colTab[0:WPT, k, q:q + 1],
                                     ident[0:WPT, 0:WPT], start=True, stop=True)
                for t in range(GT):
                    last = nc.tensor.matmul(bank[2][0:1, k * NG + t * GPT:k * NG + (t + 1) * GPT],
                                            gMM[0:GPT, k, t:t + 1], ident[0:GPT, 0:GPT], start=True, stop=True)
            last.then_inc(lohi_turned, 1)

            def turn_tiles(source, n0, b0=0, b1=NTB):
                for b in range(b0, b1):
                    t0, n = batch(b)
                    if b >= 2:
                        pe.wait_ge(res_ready if n0 > NTB * ROUNDS else t_out,
                                   b - 1 if n0 > NTB * ROUNDS else n0 + b - 1)
                    for t in range(n):
                        last = nc.tensor.transpose(bank[6 + b % 2][:, t * P:(t + 1) * P], source(t0 + t), ident[:, :])
                    last.then_inc(t_done, 1)

            pe.wait_ge(norm_ready, HI)
            turn_tiles(lambda t: h_nat[:, t, :], 0)
            pe.wait_ge(tables_ready, 1)
            pe.wait_ge(t_out, NTB)

            regs = entry_regs(pe, "pe")

            def further_edges(i):
                span = read4(pe, regs, spanTab[0:1, bass.ds(i, 1), :], WPB)
                for c in range(2):
                    with pe.If(span[2 * c + 1] > 0):
                        with pe.Fori(span[2 * c], span[2 * c + 1]) as v:
                            w = i * WPTURN + c * WPB + v
                            nx = pe.value_load(furtherTab[0:1, bass.ds(w, 1)], min_val=0, max_val=NCH)
                            with pe.If(nx > 0):
                                xb = pe.value_load(beforeTab[0:1, bass.ds(w, 1)], min_val=0, max_val=NCH * NWIN)
                                with pe.Fori(0, nx) as n:
                                    pe.wait_ge(xhot_ready, xb + n + 1)
                                    nc.tensor.matmul(psXC[:, 0:KEYS], xhot[0], xkey[:, 0:KEYS], start=True, stop=True)
                                    for q in range(3):
                                        last = nc.tensor.matmul(psXW[:, 0:KEYS], xhot[q + 1], xkey[:, 0:KEYS],
                                                                start=q == 0, stop=q == 2)
                                    last.then_inc(xhot_used, 1)

            def window(i, u):
                w, s = i * WPTURN + u, u % SETS
                pe.wait_ge(hot1_ready, w + 1)
                pe.wait_ge(win_out, w + 1)
                for j in range(STEP):
                    nc.tensor.matmul(psWin[s][:, 0:KEYS], hot[s][0][:, j, :], key[s][:, j, 0:KEYS],
                                     start=j == 0, stop=j == STEP - 1)
                pe.wait_ge(hot2_ready, w + 1)
                pe.wait_ge(hot3_ready, w + 1)
                for j in range(STEP):
                    for q in range(3):
                        last = nc.tensor.matmul(psWin[s][:, KEYS:2 * KEYS], hot[s][q + 1][:, j, :], key[s][:, j, 0:KEYS],
                                                start=j == 0 and q == 0, stop=j == STEP - 1 and q == 2)
                last.then_inc(win_done, 1)

            def further_groups(i):
                for r in range(ERING):
                    g = i * ERING + r
                    nx = pe.value_load(grpFurther[0:1, bass.ds(g, 1)], min_val=0, max_val=N // SW)
                    with pe.If(nx > 0):
                        xb = pe.value_load(grpBefore[0:1, bass.ds(g, 1)], min_val=0, max_val=NG * (N // SW))
                        with pe.Fori(0, nx) as n:
                            pe.wait_ge(e_in[r], i * 16 + 16)
                            pe.wait_ge(exhot_ready, xb + n + 1)
                            for j in range(GJ):
                                last = nc.tensor.matmul(psXC[0:EA, 0:SW], ebuf[:, r, j, :], exhot[:, j, :],
                                                        start=j == 0, stop=j == GJ - 1)
                            last.then_inc(ex_done, 1)

            def look_further(i):
                return pe.value_load(turnTab[0:1, bass.ds(i, 1)], min_val=0, max_val=MOST)

            def further_work(i, any_further):
                with pe.If(any_further > 0):
                    further_edges(i)
                    if not isinstance(i, int):
                        groups_further = pe.value_load(groupTab[0:1, bass.ds(i, 1)], min_val=0, max_val=MOST)
                        with pe.If(groups_further > 0):
                            further_groups(i)

            def group(i, r):
                g = i * ERING + r
                pe.wait_ge(e_in[r], i * 16 + 16)
                pe.wait_ge(ehot_ready, g + 1)
                pe.wait_ge(e_added, g - 1 + AHEAD)
                for j in range(GJ):
                    last = nc.tensor.matmul(psE[r % 2][0:EA, r // 2 * SW:(r // 2 + 1) * SW], ebuf[:, r, j, :],
                                            ehot[r][:, j, :], start=j == 0, stop=j == GJ - 1)
                last.then_inc(e_used, 1)

            def first_product(parity, u):
                left = WPTURN - FIRST_FROM
                for s in range((u - FIRST_FROM) * HI // left, (u + 1 - FIRST_FROM) * HI // left):
                    last = nc.tensor.matmul(psFirst[:, 0:FIRST], h_nat[:, s, :], stage[parity][:, :, 0, s, :],
                                            start=s == 0, stop=s == HI - 1)
                if u == WPTURN - 1:
                    last.then_inc(first_done, 1)

            def first_product_may_start(i):
                pe.wait_ge(turn_ready, i + 1)
                pe.wait_ge(win_out, i * WPTURN + SETS)
                pe.wait_ge(first_out, i + 1)

            pe.wait_ge(zeros_ready, 1)
            nc.tensor.matmul(psFirst[:, 0:FIRST], h_nat[:, 0, :], stage[1][:, :, 0, 0, :],
                             start=True, stop=True).then_inc(first_done, 1)
            with pe.Fori(0, NBODY // 2) as ii:
                for parity in range(2):
                    i = ii * 2 + parity
                    for u in range(WPTURN):
                        window(i, u)
                        if u == FURTHER_AT:
                            any_further = look_further(i)
                        if u in GROUP_AT:
                            group(i, GROUP_AT.index(u))
                        if u == FURTHER_AT:
                            further_work(i, any_further)
                        if u == FIRST_FROM:
                            first_product_may_start(i)
                        if u >= FIRST_FROM:
                            first_product(1 - parity, u)
            further_work(NBODY, look_further(NBODY))
            first_product_may_start(NBODY)
            for u in range(FIRST_FROM, WPTURN):
                first_product(1, u)

            pe.wait_ge(e_added, NG + AHEAD)
            pe.wait_ge(first_out, NBODY + 2)
            for j in range(NHALF):
                if j >= 2:
                    pe.wait_ge(deg_out, j - 1)
                nc.tensor.matmul(bank[6 + j % 2][:, 0:HALF], ones[FE:FE + 1, :],
                                 sumE[FE:FE + 1, j * HALF:(j + 1) * HALF], start=True, stop=True).then_inc(deg_spread, 1)
            pe.wait_ge(deg_out, NHALF)

            def product(J, c, h_rows=None):
                pe.wait_ge(strm_in[c], 8 * (J - c - NHALF) + 16)
                wait(pe, prod_out, J - 1)
                for s in range(HI):
                    if h_rows is not None:
                        h_rows(s)
                    last = nc.tensor.matmul(psP[c][:, 0:HALF], h_nat[:, s, :], strm[c][:, :, s, :],
                                            start=s == 0, stop=s == HI - 1)
                last.then_inc(prod_done, 1)

            def message(j, J, c, first=False):
                sums = firstAgg[:, bass.ds(2 * FIRST + j * HALF, HALF)] if first else agg0[c][:, :]
                pe.wait_ge(prod_out, J + 1)
                pe.wait_ge(hdeg_ready, J + 1)
                wait(pe, agg_ready, J)
                nc.tensor.matmul(psM[:, 0:HALF], wts[:, 1, :], sums, start=True, stop=False)
                nc.tensor.matmul(psM[:, 0:HALF], wts[:, 0, :], hdeg[c][:, :], start=False, stop=False)
                nc.tensor.matmul(psM[:, 0:HALF], wts[0:EA, 2, :], sumE[0:EA, bass.ds(j * HALF, HALF)],
                                 start=False, stop=True).then_inc(msg_done, 1)

            def gru(j, J, c):
                pe.wait_ge(agg_ready, J + 1)
                cols = bass.ds(j * HALF, HALF)
                pe.wait_ge(rz_ready, J + AHEAD)
                for g, ps in ((0, psR), (1, psZ)):
                    nc.tensor.matmul(ps[:, 0:HALF], wts[:, 3 + g, :], agg[c][:, :], start=True, stop=False)
                    nc.tensor.matmul(ps[:, 0:HALF], wts[:, 6 + g, :], hT[:, cols], start=False, stop=True)
                pe.wait_ge(cand_in, J + AHEAD)
                nc.tensor.matmul(psI[:, 0:HALF], wts[:, 5, :], agg[c][:, :], start=True, stop=True)
                nc.tensor.matmul(psH[:, 0:HALF], wts[:, 8, :], hT[:, cols], start=True, stop=True).then_inc(gates_done, 1)

            def turn_h(k, b0, b1):
                for b in range(b0, b1):
                    t0, n = batch(b)
                    halves = min(-(-(t0 + n) * P // HALF), NHALF)
                    pe.wait_ge(h_ready, k * NHALF + halves + AHEAD)
                    if b >= 4:
                        pe.wait_ge(t_out, NTB * (k + 1) + b - 1)
                    for t in range(n):
                        last = nc.tensor.transpose(bank[TURN_BANK[b]][:, t * P:(t + 1) * P],
                                                   hT[:, (t0 + t) * P:(t0 + t + 1) * P], ident[:, :])
                    last.then_inc(t_done, 1)

            def turn_weights(k):
                pe.wait_ge(w_prep, k + 1)
                pe.wait_ge(h_ready, k * NHALF + AHEAD)
                raw = [unat[:, 0:F], unat[:, F:2 * F], eaw[:, :]] + [ihnat[:, g, :] for g in range(3)] + \
                      [hhnat[:, g, :] for g in range(3)]
                for n, m in enumerate(raw):
                    last = nc.tensor.transpose(bank[3 + n // 3][:, n % 3 * F:(n % 3 + 1) * F], m, ident[:, :])
                    if n % 3 == 2:
                        last.then_inc(w_turned, 1)

            turn_weights(0)
            for k in range(ROUNDS):
                J = k * NHALF
                if k == 0:
                    pe.sem_inc(prod_done, NHALF)
                else:
                    product(J, 0, lambda s: pe.wait_ge(t_out, NTB * k + s // 4 + 1))
                    product(J + 1, 1)
                pe.wait_ge(w_ready, 3 * (k + 1))
                message(0, J, 0, k == 0)
                with pe.Fori(1, NSUP) as i:
                    for c in range(2):
                        if k > 0:
                            product(i * 2 + (J + c), c)
                        message(i * 2 + (c - 1), i * 2 + (J + c - 1), 1 - c, k == 0)
                        gru(i * 2 + (c - 2), i * 2 + (J + c - 2), c)
                J += NHALF
                message(NHALF - 1, J - 1, 1, k == 0)
                gru(NHALF - 2, J - 2, 0)
                gru(NHALF - 1, J - 1, 1)
                turn_h(k, 0, 4)
                if k + 1 < ROUNDS:
                    turn_weights(k + 1)
                turn_h(k, 4, NTB)

            J = ROUNDS * NHALF
            product(J, 0, lambda s: pe.wait_ge(norm_ready, HI + s + 1))
            product(J + 1, 1)
            with pe.Fori(1, NSUP - 1) as i:
                for c in range(2):
                    product(i * 2 + (J + c), c)
            product(J + NHALF - 2, 0)
            pe.wait_ge(prod_out, J + NHALF - 2)
            early = (NHALF - 2) * HALF // (4 * P)
            turn_tiles(lambda t: hT[:, t * P:(t + 1) * P], NTB * (ROUNDS + 1), 0, early)
            product(J + NHALF - 1, 1)
            pe.wait_ge(prod_out, J + NHALF)
            turn_tiles(lambda t: hT[:, t * P:(t + 1) * P], NTB * (ROUNDS + 1), early, NTB)

    return nc


_ORDER = ["x", "src", "dst", "edge_attr_64", "edge_weight", "edge_weight_n2", "L0_gnn_cond", "L0_gnn_U_W", "L0_gnn_U_b",
          "L0_gnn_Wih", "L0_gnn_Whh", "L0_gnn_bih", "L0_gnn_bhh", "L1_gnn_decay_lam"]


def kernel(**inputs):
    import numpy as np
    import concourse.bacc as bacc
    from concourse.bass_utils import run_bass_kernel_spmd

    nc = bacc.Bacc("TRN2", target_bir_lowering=False, num_devices=1)
    arrays, args = {}, []
    for name in _ORDER:
        a = np.ascontiguousarray(inputs[name])
        arrays[f"in_{name}"] = a
        args.append(nc.dram_tensor(f"in_{name}", a.shape, mybir.dt.from_np(a.dtype), kind="ExternalInput").ap())
    out = nc.dram_tensor("out", (N, F), mybir.dt.float32, kind="ExternalOutput").ap()
    build(nc, *args, out)
    r = run_bass_kernel_spmd(nc, [arrays], core_ids=[0])
    return r.results[0]["out"]
```
